# Optimizing a Trainium2 kernel written in Bass

```python
import numpy as np
import jax
import jax.numpy as jnp

def _softmax(x, axis=-1):
    return jax.nn.softmax(x, axis=axis)

def _gelu(x):
    return jax.nn.gelu(x, approximate=True)

def _silu(x):
    return jax.nn.silu(x)

def _sigmoid(x):
    return jax.nn.sigmoid(x)

def _layernorm(x, axis=-1, eps=1e-05):
    m = jnp.mean(x, axis=axis, keepdims=True)
    v = jnp.var(x, axis=axis, keepdims=True)
    return (x - m) / jnp.sqrt(v + eps)

def _scatter_add(tgt, idx, src, axis=0):
    return tgt.at[idx].add(src)

def _segment_sum(src, seg, n):
    return jax.ops.segment_sum(src, seg, n)
kernel_name = 'mk_seq_postln_d1_jaxref_r8_e9314e'

def setup_inputs(seed: int=0):
    np.random.seed(seed)
    _w = jnp.asarray

    def _L0_attn_setup():
        import jax, jax.numpy as jnp
        import numpy as np
        CHUNK = 64
        HEADS = 16

        def _chunk_mask(T, cs):
            idx = jnp.arange(T)
            blk = idx // cs * cs
            qb = blk[:, None]
            kb = blk[None, :]
            masked = (qb >= kb) & (idx[None, :] - idx[:, None] - 2 * (kb - qb) >= 1)
            return masked
        key = jax.random.key(seed)
        ks = jax.random.split(key, 6)
        B, T, C = (2, 256, 128)
        w = 0.02
        return {'x': jax.random.normal(ks[0], (B, T, C), jnp.float32), 'Wq': jax.random.normal(ks[1], (C, C), jnp.float32) * w, 'bq': jnp.zeros((C,), jnp.float32), 'Wk': jax.random.normal(ks[2], (C, C), jnp.float32) * w, 'bk': jnp.zeros((C,), jnp.float32), 'Wv': jax.random.normal(ks[3], (C, C), jnp.float32) * w, 'bv': jnp.zeros((C,), jnp.float32), 'Wo': jax.random.normal(ks[4], (C, C), jnp.float32) * w, 'bo': jnp.zeros((C,), jnp.float32), 'attn_scale': jnp.full((1,), 1.0 / np.sqrt(C // HEADS), jnp.float32)}
    _L0_attn_in = _L0_attn_setup()

    def _L0_ffn_setup():
        import jax, jax.numpy as jnp
        import numpy as np
        H = 128
        I = 64
        E = 32
        TOP_K = 6
        N_GROUP = 8
        TOPK_GROUP = 4
        SCALE = 2.5
        N_SHARED = 2
        SI = I * N_SHARED
        B, S = (2, 128)
        key = jax.random.key(seed)
        ks = jax.random.split(key, 8)
        x = jax.random.normal(ks[0], (B, S, H), jnp.float32)
        gate_weight = jax.random.normal(ks[1], (E, H), jnp.float32) * 0.02
        e_score_correction_bias = jax.random.normal(ks[2], (E,), jnp.float32) * 0.01
        experts_gate_up = jax.random.normal(ks[3], (E, 2 * I, H), jnp.float32) * 0.02
        experts_down = jax.random.normal(ks[4], (E, H, I), jnp.float32) * 0.02
        shared_gate_w = jax.random.normal(ks[5], (SI, H), jnp.float32) * 0.02
        shared_up_w = jax.random.normal(ks[6], (SI, H), jnp.float32) * 0.02
        shared_down_w = jax.random.normal(ks[7], (H, SI), jnp.float32) * 0.02
        return {'x': x, 'gate_weight': gate_weight, 'e_score_correction_bias': e_score_correction_bias, 'experts_gate_up': experts_gate_up, 'experts_down': experts_down, 'shared_gate_w': shared_gate_w, 'shared_up_w': shared_up_w, 'shared_down_w': shared_down_w}
    _L0_ffn_in = _L0_ffn_setup()
    _d = {'L0_attn_x': _L0_attn_in['x'], 'L0_attn_Wq': _L0_attn_in['Wq'], 'L0_attn_bq': _L0_attn_in['bq'], 'L0_attn_Wk': _L0_attn_in['Wk'], 'L0_attn_bk': _L0_attn_in['bk'], 'L0_attn_Wv': _L0_attn_in['Wv'], 'L0_attn_bv': _L0_attn_in['bv'], 'L0_attn_Wo': _L0_attn_in['Wo'], 'L0_attn_bo': _L0_attn_in['bo'], 'L0_attn_attn_scale': _L0_attn_in['attn_scale'], 'L0_ffn_gate_weight': _L0_ffn_in['gate_weight'], 'L0_ffn_e_score_correction_bias': _L0_ffn_in['e_score_correction_bias'], 'L0_ffn_experts_gate_up': _L0_ffn_in['experts_gate_up'], 'L0_ffn_experts_down': _L0_ffn_in['experts_down'], 'L0_ffn_shared_gate_w': _L0_ffn_in['shared_gate_w'], 'L0_ffn_shared_up_w': _L0_ffn_in['shared_up_w'], 'L0_ffn_shared_down_w': _L0_ffn_in['shared_down_w']}
    _x0 = _d['L0_attn_x']
    _d['L0_attn_x'] = jax.random.normal(jax.random.fold_in(jax.random.key(seed), 1), (2, 1024, 128), dtype=_x0.dtype)
    del _x0
    return _d

def reference(L0_attn_x, L0_attn_Wq, L0_attn_bq, L0_attn_Wk, L0_attn_bk, L0_attn_Wv, L0_attn_bv, L0_attn_Wo, L0_attn_bo, L0_attn_attn_scale, L0_ffn_gate_weight, L0_ffn_e_score_correction_bias, L0_ffn_experts_gate_up, L0_ffn_experts_down, L0_ffn_shared_gate_w, L0_ffn_shared_up_w, L0_ffn_shared_down_w):

    def _L0_attn_ref(x, Wq, bq, Wk, bk, Wv, bv, Wo, bo, attn_scale):
        import jax, jax.numpy as jnp
        import numpy as np
        CHUNK = 64
        HEADS = 16

        def _chunk_mask(T, cs):
            idx = jnp.arange(T)
            blk = idx // cs * cs
            qb = blk[:, None]
            kb = blk[None, :]
            masked = (qb >= kb) & (idx[None, :] - idx[:, None] - 2 * (kb - qb) >= 1)
            return masked
        B, T, C = x.shape
        H = HEADS
        D = C // H
        q = (x @ Wq.T + bq).reshape(B, T, H, D)
        k = (x @ Wk.T + bk).reshape(B, T, H, D)
        v = (x @ Wv.T + bv).reshape(B, T, H, D)
        scores = jnp.einsum('bqhd,bkhd->bhqk', q, k) * attn_scale[0]
        mask = _chunk_mask(T, CHUNK)
        scores = jnp.where(mask[None, None], -jnp.inf, scores)
        attn = jax.nn.softmax(scores, axis=-1)
        out = jnp.einsum('bhqk,bkhd->bqhd', attn, v).reshape(B, T, C)
        return out @ Wo.T + bo

    def _L0_ffn_ref(x, gate_weight, e_score_correction_bias, experts_gate_up, experts_down, shared_gate_w, shared_up_w, shared_down_w):
        import jax, jax.numpy as jnp
        import numpy as np
        H = 128
        I = 64
        E = 32
        TOP_K = 6
        N_GROUP = 8
        TOPK_GROUP = 4
        SCALE = 2.5
        N_SHARED = 2
        SI = I * N_SHARED
        B, S = (2, 128)
        b, s, h = x.shape
        xf = x.reshape(-1, h)
        T = xf.shape[0]
        logits = xf.astype(jnp.float32) @ gate_weight.astype(jnp.float32).T
        scores = jax.nn.sigmoid(logits)
        sfc = scores + e_score_correction_bias[None, :]
        gs = E // N_GROUP
        group_scores = sfc.reshape(T, N_GROUP, gs).max(axis=-1)
        _, gidx = jax.lax.top_k(group_scores, TOPK_GROUP)
        gmask = jnp.zeros((T, N_GROUP), bool).at[jnp.arange(T)[:, None], gidx].set(True)
        smask = jnp.repeat(gmask, gs, axis=1)
        masked = jnp.where(smask, sfc, 0.0)
        _, topk_idx = jax.lax.top_k(masked, TOP_K)
        tw = jnp.take_along_axis(scores, topk_idx, axis=1)
        tw = tw / (tw.sum(-1, keepdims=True) + 1e-20)
        tw = (tw * SCALE).astype(xf.dtype)
        combine = jnp.zeros((T, E), xf.dtype).at[jnp.arange(T)[:, None], topk_idx].add(tw)

        def expert_step(acc, inp):
            gu, dn, c = inp
            g = xf @ gu[:I].T
            u = xf @ gu[I:].T
            o = jax.nn.silu(g) * u @ dn.T
            return (acc + c[:, None] * o, None)
        routed, _ = jax.lax.scan(expert_step, jnp.zeros_like(xf), (experts_gate_up, experts_down, combine.T))
        sh = jax.nn.silu(xf @ shared_gate_w.T) * (xf @ shared_up_w.T)
        shared_out = sh @ shared_down_w.T
        return (routed + shared_out).reshape(b, s, h)
    x = L0_attn_x
    x = _layernorm(x + _L0_attn_ref(x, L0_attn_Wq, L0_attn_bq, L0_attn_Wk, L0_attn_bk, L0_attn_Wv, L0_attn_bv, L0_attn_Wo, L0_attn_bo, L0_attn_attn_scale), axis=-1)
    x = _layernorm(x + _L0_ffn_ref(x, L0_ffn_gate_weight, L0_ffn_e_score_correction_bias, L0_ffn_experts_gate_up, L0_ffn_experts_down, L0_ffn_shared_gate_w, L0_ffn_shared_up_w, L0_ffn_shared_down_w), axis=-1)
    return x

_drawn_inputs = setup_inputs


def setup_inputs(seed=0):
    import zlib

    import numpy as np

    out = dict(_drawn_inputs(seed))
    spreads = {'L0_attn_bq': (0.0, 0.8),
     'L0_attn_bk': (0.0, 0.8),
     'L0_attn_bv': (0.0, 0.384),
     'L0_attn_bo': (0.0, 0.1)}
    factors = {'L0_attn_Wq': 8.0,
     'L0_attn_Wk': 8.0,
     'L0_attn_Wv': 8.0,
     'L0_ffn_gate_weight': 8.0,
     'L0_ffn_e_score_correction_bias': 8.0,
     'L0_ffn_experts_gate_up': 8.0,
     'L0_ffn_experts_down': 8.0,
     'L0_ffn_shared_gate_w': 8.0,
     'L0_ffn_shared_up_w': 8.0,
     'L0_ffn_shared_down_w': 8.0}
    for name, (base, spread) in spreads.items():
        noise = np.random.default_rng([zlib.crc32(name.encode()), seed]).standard_normal(out[name].shape)
        drawn = base * np.exp(spread * noise) if base else spread * noise
        out[name] = jnp.asarray(drawn.astype(out[name].dtype))
    for name, factor in factors.items():
        out[name] = (out[name] * factor).astype(out[name].dtype)
    return out
```

```python
import concourse.bass as bass
from concourse import mybir
from concourse.alu_op_type import AluOpType as ALU
from contextlib import ExitStack

P = 128
B, T, C = 2, 1024, 128
HEADS, D = 16, 8
CHUNK = 64
E, I, TOP_K = 32, 64, 6
N_GROUP, TOPK_GROUP = 8, 4
ROUTE_SCALE = 2.5
EPS = 1e-5
BANK = 512

NTOK = B * T
NT = NTOK // P
NC = NTOK // BANK
KT = T // P
HG = 4
GPB = HEADS // HG
NG = B * GPB
STRIP = P // HG
NS = 3
NPAIR = E // 2
NU = NPAIR + 1

ROWS_QK = 48
MROW = 96
K_MAX = 72
K_EXP = MROW + 3


def max_units():
    units = []
    for qt in range(KT - 1, -1, -1):
        n = T - P * qt
        for part, (k0, m) in enumerate([(P * qt, min(n, BANK)), (P * qt + BANK, n - BANK)]):
            if m <= 0:
                continue
            per = BANK // m if BANK % m == 0 else 1
            for j in range(0, HG, per):
                units.append(([(j + a, qt, k0, m, a * m) for a in range(per)], m, part))
    return units


def exp_units():
    units = []
    for kt in range(KT - 1, -1, -1):
        n = P * (kt + 1)
        if n > BANK:
            per, stride = 1, 2 * BANK
        elif 2 * n > BANK:
            per, stride = 2, BANK
        else:
            per, stride = 4, n
        units += [(kt, j, per, stride) for j in range(0, HG, per)]
    return units


MAXU, EXPU = max_units(), exp_units()
NM = len(MAXU) + 1
NE = len(EXPU)
EXPS_UP_TO = {kt: sum(u[0] >= kt for u in EXPU) for kt in range(KT)}


def build(nc, a, out):
    f32, bf16, f32r = mybir.dt.float32, mybir.dt.bfloat16, mybir.dt.float32r
    u32 = mybir.dt.uint32
    ACT, AX = mybir.ActivationFunctionType, mybir.AxisListType
    ctx = ExitStack()
    with ctx:
        def sb(name, shape, dt):
            return ctx.enter_context(nc.sbuf_tensor(name, shape, dt))

        def sem(name):
            return ctx.enter_context(nc.semaphore(name))

        ident = sb("ident", [P, P], f32)
        identb = sb("identb", [P, P], bf16)
        mask_qk = sb("mask_qk", [P, P], bf16)
        mask_kq = sb("mask_kq", [P, P], bf16)
        small = sb("small", [P, E + N_GROUP * N_GROUP], f32)
        wq, wk, wv, wo = (sb(n, [P, C], f32) for n in ("wq", "wk", "wv", "wo"))
        bq, bk, bqs = (sb(n, [P, 1], f32) for n in ("bq", "bk", "bqs"))
        scale = sb("scale", [P, 1], f32)
        bvb, bob = sb("bvb", [P, C], f32), sb("bob", [P, C], f32)
        ebias = sb("ebias", [P, E], f32)
        gate_w = sb("gate_w", [P, E], f32)
        gu_raw = sb("gu_raw", [P, 2, 2 * P], f32)
        gu_hi = sb("gu_hi", [P, NU, 2 * P], f32r)
        gu_lo = sb("gu_lo", [P, NU, 2 * P], f32r)
        down = sb("down", [P, NU, C], f32)
        x = sb("x", [P, NT, C], f32)
        with ExitStack() as early:
            xT, V = (early.enter_context(nc.sbuf_tensor(n, [P, NTOK], f32)) for n in ("xT", "V"))
        V = V[:, :].rearrange("p (t c) -> p t c", c=C)
        x1hi, x1lo = (sb(n, [P, NTOK], f32r) for n in ("x1hi", "x1lo"))
        Vg = sb("Vg", [P, 2, KT, HG, STRIP], f32)
        rows_q = sb("rows_q", [P, NS, HG * T], bf16)
        rows_k = sb("rows_k", [P, NS, HG * T], bf16)
        probs = sb("probs", [P, 2, HG * T], f32)
        mx = sb("mx", [P, 2, HG, KT], f32)
        mh = sb("mh", [HG * KT, 3, P], bf16)
        mr = sb("mr", [HG * KT, P], f32)
        oT = sb("oT", [P, NG, T], f32)
        q32 = oT[:, 0, :].rearrange("p (s n) -> p s n", s=2)
        r32 = oT[:, 1, :].rearrange("p (s n) -> p s n", s=2)
        parts = oT[:, 2:4, :].bitcast(bf16).rearrange("p s (h n) -> p s h n", n=BANK)
        x1 = sb("x1", [P, NT, C], f32)
        rec = sb("rec", [P, 2, HEADS], f32)
        att = sb("att", [P, 2, C], f32)
        attT = sb("attT", [P, 2, C], f32)
        stats = sb("stats", [P, NT, 6], f32)
        mv = sb("mv", [P, NT, 2], f32)
        ve = sb("ve", [P, NT], f32)
        half = sb("half", [P, NT], f32)
        rstd = sb("rstd", [P, NT], f32)
        sg = probs[:, 0, NTOK:NTOK + 2 * BANK].rearrange("p (s n) -> p s n", s=2)
        au = probs[:, 0, NTOK + 2 * BANK:].rearrange("p (s n) -> p s n", s=2)
        hh = probs[:, 1, 0:2 * BANK].rearrange("p (s n) -> p s n", s=2)
        moT = probs[:, 1, 2 * BANK:4 * BANK].rearrange("p (s n) -> p s n", s=2)
        yy = probs[:, 1, 4 * BANK:].rearrange("p (s t n) -> p s t n", s=4, n=C)
        rk = rows_k[:, 0, :].bitcast(f32)
        sc, sfc = rk[:, 0:512], rk[:, 512:1024]
        msk, comb = rk[:, 1024:1536], rk[:, 1536:2048]
        rk1 = rows_k[:, 1, :].bitcast(f32)
        cmp_gt, cmp_eq = rk1[:, 0:1024], rk1[:, 1024:2048]
        one_hot = oT[:, 0:3, :].rearrange("p a b -> p (a b)")
        gs, rank = (oT[:, 5, k * P:(k + 1) * P] for k in range(2))
        m8 = oT[:, 5, 2 * P:3 * P].rearrange("p (t k) -> p t k", k=8)
        i8 = oT[:, 5, 4 * P:5 * P].bitcast(u32).rearrange("p (t k) -> p t k", k=8)
        i8f = oT[:, 5, 3 * P:4 * P].rearrange("p (t k) -> p t k", k=8)
        csum, cs2 = sb("csum", [P, NT], f32), sb("cs2", [P, NT], f32)
        cpart = rows_q[:, 0, 0:NT * 3 * E].rearrange("p (t h e) -> p t h e", h=3, e=E)
        cres = oT[:, 4, 0:512]
        combT = rows_q[0:3 * E, 1, 0:NTOK]
        sel = rows_q[0:3 * E, 2, 0:NPAIR * P]
        gate_hi, gate_lo = sb("gate_hi", [P, E], f32r), sb("gate_lo", [P, E], f32r)

        ps = ctx.enter_context(nc.psum_tensor("ps", [P, 8 * BANK], f32))

        def bank(n, cols=BANK, at=0):
            return ps[:, n * BANK + at:n * BANK + at + cols]

        s_w = sem("s_w")
        s_xt = [sem(f"s_xt{n}") for n in range(NC)]
        s_c = sem("s_c")
        s_c2 = sem("s_c2")
        s_mw = sem("s_mw")
        s_gw = [sem("s_gw0"), sem("s_gw1")]
        s_bqs = sem("s_bqs")
        s_pj = sem("s_pj")
        s_q32 = sem("s_q32")
        s_split = sem("s_split")
        s_parts = sem("s_parts")
        s_scr = [sem("s_scr0"), sem("s_scr1")]
        s_vp = sem("s_vp")
        s_v = sem("s_v")
        s_zero = sem("s_zero")
        s_rows = [sem(f"s_rows{n}") for n in range(NS)]
        s_mrow = [sem(f"s_mrow{n}") for n in range(NS)]
        s_sm = sem("s_sm")
        s_mxd = sem("s_mxd")
        s_mxc = sem("s_mxc")
        s_mc = sem("s_mc")
        s_mh = sem("s_mh")
        s_st = sem("s_st")
        s_ex = sem("s_ex")
        s_vg = sem("s_vg")
        s_pv = sem("s_pv")
        s_ea = sem("s_ea")
        s_gs = sem("s_gs")
        s_t1, s_rc, s_at, s_t2, s_aT, s_wo = (sem(n) for n in ("s_t1", "s_rc", "s_at", "s_t2", "s_aT", "s_wo"))
        s_r, s_bn, s_mv, s_ve, s_rs, s_hf, s_x1 = (sem(n) for n in ("s_r", "s_bn", "s_mv", "s_ve", "s_rs", "s_hf", "s_x1"))
        s_t3, s_hi, s_lo, s_lg, s_sig, s_rt, s_cp, s_ct, s_cT = (
            sem(n) for n in ("s_t3", "s_hi", "s_lo", "s_lg", "s_sig", "s_rt", "s_cp", "s_ct", "s_cT"))
        s_g, s_u, s_cb, s_sg, s_au, s_hh, s_dn, s_mo, s_t4 = (
            sem(n) for n in ("s_g", "s_u", "s_cb", "s_sg", "s_au", "s_hh", "s_dn", "s_mo", "s_t4"))
        s_y, s_out, s_xb, s_gl = sem("s_y"), sem("s_out"), sem("s_xb"), sem("s_gl")

        scr = a["scratch"]

        def pairs(i):
            return i - i // NU

        def wait_read(eng, i):
            if i % NU < NPAIR:
                eng.wait_ge(s_au, pairs(i + 1))
            else:
                eng.wait_ge(s_hh, i + 1)

        block = ctx.enter_context(nc.Block())

        @block.sync
        def _(sp):
            sp.dma_start(wq[:, :], a["wqT"]).then_inc(s_w, 16)
            sp.dma_start(wk[:, :], a["wkT"]).then_inc(s_w, 16)
            sp.dma_start(bq[:, :], a["bq"]).then_inc(s_w, 16)
            sp.dma_start(bk[:, :], a["bk"]).then_inc(s_w, 16)
            sp.dma_start(scale[:, :], a["attn_scale"].to_broadcast([P, 1])).then_inc(s_w, 16)
            for n in range(NC):
                sp.dma_start(xT[:, n * BANK:(n + 1) * BANK], a["xT"][:, n * BANK:(n + 1) * BANK]).then_inc(s_xt[n], 16)
            sp.dma_start(wv[:, :], a["wvT"]).then_inc(s_c, 16)
            sp.dma_start(bvb[:, :], a["bv"].to_broadcast([P, C])).then_inc(s_c, 16)
            sp.dma_start(identb[:, :], a["ident_bf16"]).then_inc(s_c, 16)
            sp.dma_start(mask_qk[:, :], a["mask_qk"]).then_inc(s_c, 16)
            sp.dma_start(mask_kq[:, :], a["mask_kq"]).then_inc(s_c, 16)
            sp.dma_start(ident[:, :], a["ident"]).then_inc(s_c, 16)
            for n in range(2 * NC):
                q_or_k, n4 = n % 2, n // 2
                sp.wait_ge(s_parts, n + 1)
                half_batch = slice((n4 % 2) * BANK, (n4 % 2 + 1) * BANK)
                sp.dma_start(scr[q_or_k, n4 // 2][:, :, half_batch].rearrange("h c t -> c h t"),
                             parts[:, n % 2, 0:3, :]).then_inc(s_scr[n % 2], 16)

            def load_rows(g):
                b, r = g // GPB, slice((g % GPB) * STRIP, (g % GPB + 1) * STRIP)
                s = g % NS
                for which, dst, reps in ((0, rows_q, None), (1, rows_k, 3)):
                    part = scr[which, b, :, r, :].rearrange("h (d j) t -> h d (j t)", d=D)
                    if reps is None:
                        spans = ((0, 24, part), (24, 16, part[0:2]), (40, 8, part[0]))
                    else:
                        spans = ((0, 24, part[0:1].to_broadcast([3, D, HG * T])),
                                 (24, 16, part[1:2].to_broadcast([2, D, HG * T])), (40, 8, part[2]))
                    for at, n, src in spans:
                        sp.dma_start(dst[at:at + n, s, :], src).then_inc(s_rows[s], 16)

            for s in range(2):
                sp.wait_ge(s_scr[s], 16 * NC)
            sp.wait_ge(s_zero, 3 * NS)
            for g in range(NS):
                load_rows(g)
            sp.dma_start(x[:, :, :], a["x"].rearrange("(n p) c -> p n c", p=P)).then_inc(s_c2, 16)
            sp.dma_start(wo[:, :], a["woT"]).then_inc(s_c2, 16)
            sp.dma_start(bob[:, :], a["bo"].to_broadcast([P, C])).then_inc(s_c2, 16)
            sp.dma_start(gate_w[:, :], a["gateT"]).then_inc(s_c2, 16)
            sp.dma_start(ebias[:, :], a["ebias"].to_broadcast([P, E])).then_inc(s_c2, 16)
            sp.dma_start(small[:, :], a["small"]).then_inc(s_c2, 16)
            sp.dma_start(down[:, :, :], a["downT"]).then_inc(s_mw, 16)

            def load_unit(u):
                if u >= 2:
                    sp.wait_ge(s_gs, 2 * (u - 1))
                sp.dma_start(gu_raw[:, u % 2, :], a["guT"][:, u, :]).then_inc(s_gw[u % 2], 16)

            def store_max(g):
                s = g % NS
                sp.wait_ge(s_mh, g + 1)
                for h in range(3):
                    sp.dma_start(rows_q[MROW + h:MROW + h + 1, s, :], mh[:, h, :]).then_inc(s_mrow[s], 16)

            u = 0
            for g in range(NG):
                store_max(g)
                if 1 <= g <= NG - NS:
                    sp.wait_ge(s_st, NE * g)
                    load_rows(g + NS - 1)
                for _ in range(3):
                    if u < NU:
                        load_unit(u)
                        u += 1

            sp.wait_ge(s_st, NE * NG)
            sp.dma_start(sel, a["sel"]).then_inc(s_mw, 16)
            for n in range(NC):
                sp.wait_ge(s_y, 4 * (n + 1))
                sp.dma_start(out[n * BANK:(n + 1) * BANK, :].rearrange("(t p) c -> p t c", p=P),
                             yy[:, n % 4, :, :]).then_inc(s_out, 16)
            sp.wait_ge(s_out, 16 * NC)

        @block.gpsimd
        def _(pool):
            for s in range(NS):
                pool.memset(rows_q[0:MROW, s, :].bitcast(f32), 0.0).then_inc(s_zero, 1)
                pool.memset(rows_k[0:MROW, s, :].bitcast(f32), 0.0).then_inc(s_zero, 1)
                pool.wait_ge(s_zero, 3 * s + 2)
                pool.memset(rows_k[MROW:P, s, :], 1.0).then_inc(s_zero, 1)
                pool.wait_ge(s_zero, 3 * s + 3)
            pool.memset(half[:, :], -0.5).then_inc(s_hf, 1)
            pool.memset(Vg[:, :, :, :, :], 0.0).then_inc(s_hf, 1)
            pool.wait_ge(s_hf, 2)
            pool.memset(Vg[:, :, :, :, D:D + 1], 1.0).then_inc(s_hf, 1)
            pool.wait_ge(s_hf, 3)

            def values(g):
                pool.wait_ge(s_v, 2 * (g // GPB + 1))
                if g >= 2:
                    pool.wait_ge(s_pv, KT * (g - 1))
                c0 = (g % GPB) * STRIP
                src = V[:, (g // GPB) * KT:(g // GPB + 1) * KT, c0:c0 + STRIP]
                pool.tensor_copy(Vg[:, g % 2, :, :, 0:D],
                                 src.rearrange("p k (j d) -> p k j d", d=D)).then_inc(s_vg, 1)

            u = 0
            for g in range(NG):
                values(g)
                if g == 0:
                    pool.wait_ge(s_c2, 16 * 6)
                    pool.tensor_tensor(x[:, :, :], x[:, :, :], bob[:, :].unsqueeze(1).to_broadcast([P, NT, C]),
                                       ALU.add).then_inc(s_xb, 1)
                for _ in range(3):
                    if u < NU:
                        pool.wait_ge(s_gw[u % 2], 16 * (u // 2 + 1))
                        pool.tensor_copy(gu_hi[:, u, :], gu_raw[:, u % 2, :]).then_inc(s_gs, 1)
                        pool.wait_ge(s_gs, 2 * u + 1)
                        pool.tensor_tensor(gu_lo[:, u, :], gu_raw[:, u % 2, :], gu_hi[:, u, :],
                                           ALU.subtract).then_inc(s_gs, 1)
                        u += 1
            pool.wait_ge(s_ve, 1)
            pool.tensor_tensor(rstd[:, :], ve[:, :], half[:, :], ALU.pow).then_inc(s_rs, 1)
            for n in range(NC):
                pool.wait_ge(s_ve, n + 2)
                pool.tensor_tensor(rstd[:, 4 * n:4 * n + 4], ve[:, 4 * n:4 * n + 4], half[:, 4 * n:4 * n + 4],
                                   ALU.pow).then_inc(s_rs, 1)

        @block.scalar
        def _(act):
            act.wait_ge(s_w, 80)
            act.activation(bqs[:, :], bq[:, :], ACT.Copy, scale=scale[:, 0:1]).then_inc(s_bqs, 1)
            act.wait_ge(s_bqs, 1)
            for n in range(2 * NC):
                act.wait_ge(s_pj, n + 1)
                if n >= 2:
                    act.wait_ge(s_parts, n - 1)
                    act.wait_ge(s_scr[n % 2], 16 * (n // 2))
                how = dict(scale=scale[:, 0:1], bias=bqs[:, 0:1]) if n % 2 == 0 else dict(bias=bk[:, 0:1])
                act.activation(q32[:, n % 2, :], bank(n % 2), ACT.Identity, **how).then_inc(s_q32, 1)
                act.activation(parts[:, n % 2, 0, :], bank(n % 2), ACT.Identity, **how).then_inc(s_q32, 1)

            def exponentials(g, n):
                kt, j, per, stride = EXPU[n]
                cols = P * (kt + 1)
                act.wait_ge(s_st, NE * g + n + 1)
                order = KT * g + KT - 1 - kt
                if order >= 2:
                    act.wait_ge(s_pv, order - 1)
                src = ps[:, (n % 2) * 2 * BANK:(n % 2 + 1) * 2 * BANK]
                if per > 1:
                    src = src[:, 0:per * stride].rearrange("p (j n) -> p j n", j=per)[:, :, 0:cols]
                    dst = probs[:, (KT - 1 - kt) % 2, :].rearrange("p (j n) -> p j n", j=HG)[:, j:j + per, 0:cols]
                else:
                    src = src[:, 0:cols]
                    dst = probs[:, (KT - 1 - kt) % 2, j * T:j * T + cols]
                act.activation(dst, src, ACT.Exp).then_inc(s_ex, 1)

            for g in range(NG):
                for n in range(NE):
                    exponentials(g, n)
                act.wait_ge(s_pv, KT * (g + 1))
                act.copy(oT[:, g, :], ps[:, 4 * BANK:6 * BANK]).then_inc(s_ea, 1)

            for t in range(NT):
                act.wait_ge(s_t2, t + 1)
                if t >= 2:
                    act.wait_ge(s_wo, t - 1)
                act.copy(attT[:, t % 2, :], bank(2 + t % 2, P)).then_inc(s_aT, 1)
            for n in range(NC):
                act.wait_ge(s_t3, n + 1)
                act.copy(x1hi[:, n * BANK:(n + 1) * BANK], bank(6 + n % 2)).then_inc(s_hi, 1)
            act.wait_ge(s_lg, 1)
            act.activation(sc, bank(0), ACT.Sigmoid).then_inc(s_sig, 1)
            for c in range(2):
                act.wait_ge(s_ct, c + 1)
                act.copy(combT[:, c * T:(c + 1) * T],
                         bank(2 + c)[0:3 * E, :].bitcast(bf16)).then_inc(s_cT, 1)

            def expert_sum(n):
                act.wait_ge(s_dn, NU * (n + 1))
                if n >= 2:
                    act.wait_ge(s_t4, n - 1)
                act.copy(moT[:, n % 2, :], bank(6 + n % 2)).then_inc(s_mo, 1)

            for n in range(NC):
                for u in range(NU):
                    i = NU * n + u
                    act.wait_ge(s_g, i + 1)
                    if i >= 2:
                        wait_read(act, i - 2)
                    act.activation(sg[:, i % 2, :], bank(i % 2), ACT.Silu).then_inc(s_sg, 1)
                    if n >= 1 and u == 2:
                        expert_sum(n - 1)
            expert_sum(NC - 1)

        @block.vector
        def _(dve):
            for n in range(2 * NC):
                s = n % 2
                dve.wait_ge(s_q32, 2 * n + 2)
                dve.tensor_tensor(r32[:, s, :], q32[:, s, :], parts[:, s, 0, :], ALU.subtract).then_inc(s_split, 1)
                dve.wait_ge(s_split, 2 * n + 1)
                dve.tensor_copy(parts[:, s, 1, :], r32[:, s, :]).then_inc(s_split, 1)
                dve.wait_ge(s_split, 2 * n + 2)
                dve.tensor_tensor(parts[:, s, 2, :], r32[:, s, :], parts[:, s, 1, :], ALU.subtract).then_inc(s_parts, 1)
            for n in range(NC):
                dve.wait_ge(s_vp, n + 1)
                dve.tensor_tensor(V[:, 4 * n:4 * n + 4, :], bank(2 + n % 2).rearrange("p (t c) -> p t c", c=C),
                                  bvb[:, :].unsqueeze(1).to_broadcast([P, 4, C]), ALU.add).then_inc(s_v, 1)

            def maxima(g):
                for n, (cells, m, part) in enumerate(MAXU):
                    j, qt = cells[0][:2]
                    per = len(cells)
                    dve.wait_ge(s_sm, NM * g + n + 1)
                    src = bank(6 + n % 2, per * m).rearrange("p (j m) -> p j m", j=per)
                    dve.tensor_reduce(mx[:, part, j:j + per, qt], src, AX.X, ALU.max).then_inc(s_mxd, 1)
                wide = KT - BANK // P
                dve.wait_ge(s_mxd, (NM - 1) * (g + 1))
                dve.tensor_tensor(mx[:, 0, :, 0:wide], mx[:, 0, :, 0:wide], mx[:, 1, :, 0:wide],
                                  ALU.max).then_inc(s_mxc, 1)
                if g >= 1:
                    dve.wait_ge(s_mrow[(g - 1) % NS], 48 * ((g - 1) // NS + 1))
                top = bank(6, P)[0:HG * KT, :]
                dve.wait_ge(s_sm, NM * (g + 1))
                dve.tensor_scalar(mh[:, 0, :], top, -1.0, None, ALU.mult).then_inc(s_mc, 1)
                dve.wait_ge(s_mc, 3 * g + 1)
                dve.scalar_tensor_tensor(mr[:, :], top, -1.0, mh[:, 0, :], ALU.mult, ALU.subtract).then_inc(s_mc, 1)
                dve.wait_ge(s_mc, 3 * g + 2)
                dve.tensor_copy(mh[:, 1, :], mr[:, :]).then_inc(s_mc, 1)
                dve.wait_ge(s_mc, 3 * g + 3)
                dve.tensor_tensor(mh[:, 2, :], mr[:, :], mh[:, 1, :], ALU.subtract).then_inc(s_mh, 1)

            for g in range(NG):
                maxima(g)

            def first_norm(t):
                s = t % 2
                o = bank(s).rearrange("p (h e) -> p h e", e=STRIP)
                dve.wait_ge(s_t1, t + 1)
                dve.reciprocal(rec[:, s, :], o[:, :, D]).then_inc(s_rc, 1)
                dve.wait_ge(s_rc, t + 1)
                if t >= 2:
                    dve.wait_ge(s_t2, t - 1)
                dve.tensor_tensor(att[:, s, :].rearrange("p (h d) -> p h d", d=D), o[:, :, 0:D],
                                  rec[:, s, :].unsqueeze(2).to_broadcast([P, HEADS, D]), ALU.mult).then_inc(s_at, 1)

            def residual(t):
                dve.wait_ge(s_wo, t + 1)
                dve.tensor_tensor(x1[:, t, :], bank(4 + t % 2, P), x[:, t, :], ALU.add).then_inc(s_r, 1)
                dve.wait_ge(s_r, t + 1)
                dve.bn_stats(stats[:, t, :], x1[:, t, :]).then_inc(s_bn, 1)
                dve.wait_ge(s_bn, t + 1)
                dve.bn_aggr(mv[:, t, :], stats[:, t, :]).then_inc(s_mv, 1)

            dve.wait_ge(s_c2, 16 * 6)
            dve.tensor_copy(gate_hi[:, :], gate_w[:, :]).then_inc(s_gl, 1)
            dve.wait_ge(s_gl, 1)
            dve.tensor_tensor(gate_lo[:, :], gate_w[:, :], gate_hi[:, :], ALU.subtract).then_inc(s_gl, 1)
            dve.wait_ge(s_xb, 1)
            for t in range(NT + 2):
                if t < NT:
                    first_norm(t)
                if t >= 2:
                    residual(t - 2)
            dve.wait_ge(s_mv, NT)
            dve.tensor_scalar(ve[:, :], mv[:, :, 1], EPS, None, ALU.add).then_inc(s_ve, 1)
            dve.wait_ge(s_rs, 1)
            for t in range(NT):
                dve.tensor_scalar(x1[:, t, :], x1[:, t, :], mv[:, t, 0:1], rstd[:, t:t + 1],
                                  ALU.subtract, ALU.mult).then_inc(s_x1, 1)
            for n in range(NC):
                dve.wait_ge(s_hi, n + 1)
                dve.tensor_tensor(x1lo[:, n * BANK:(n + 1) * BANK], bank(6 + n % 2),
                                  x1hi[:, n * BANK:(n + 1) * BANK], ALU.subtract).then_inc(s_lo, 1)

            count = [0]

            def link(ins):
                count[0] += 1
                ins.then_inc(s_rt, 1)
                dve.wait_ge(s_rt, count[0])

            dve.wait_ge(s_sig, 1)
            sc3, sfc3 = (v.rearrange("p (t e) -> p t e", e=E) for v in (sc, sfc))
            link(dve.tensor_tensor(sfc3, sc3, ebias[:, :].unsqueeze(1).to_broadcast([P, NT, E]), ALU.add))
            link(dve.tensor_reduce(gs, sfc.rearrange("p (g e) -> p g e", e=E // N_GROUP), AX.X, ALU.max))
            g3 = gs.rearrange("p (t g) -> p t g", g=N_GROUP)
            quad = [P, NT, N_GROUP, N_GROUP]
            other, own = g3.unsqueeze(2).to_broadcast(quad), g3.unsqueeze(3).to_broadcast(quad)
            gt4, eq4 = (v.rearrange("p (t i j) -> p t i j", i=N_GROUP, j=N_GROUP) for v in (cmp_gt, cmp_eq))
            earlier = small[:, E:].rearrange("p (i j) -> p i j", j=N_GROUP).unsqueeze(1).to_broadcast(quad)
            link(dve.tensor_tensor(gt4, other, own, ALU.is_gt))
            link(dve.tensor_tensor(eq4, other, own, ALU.is_equal))
            link(dve.tensor_tensor(eq4, eq4, earlier, ALU.mult))
            link(dve.tensor_tensor(cmp_gt, cmp_gt, cmp_eq, ALU.add))
            link(dve.tensor_reduce(rank, cmp_gt.rearrange("p (g j) -> p g j", j=N_GROUP), AX.X, ALU.add))
            link(dve.tensor_scalar(rank, rank, float(TOPK_GROUP), None, ALU.is_lt))
            per = E // N_GROUP
            link(dve.tensor_tensor(msk.rearrange("p (g e) -> p g e", e=per), sfc.rearrange("p (g e) -> p g e", e=per),
                                   rank.unsqueeze(2).to_broadcast([P, NT * N_GROUP, per]), ALU.mult))
            for t in range(NT):
                dve.max(m8[:, t, :], msk[:, t * E:(t + 1) * E]).then_inc(s_rt, 1)
            count[0] += NT
            dve.wait_ge(s_rt, count[0])
            for t in range(NT):
                dve.max_index(i8[:, t, :], m8[:, t, :], msk[:, t * E:(t + 1) * E]).then_inc(s_rt, 1)
            count[0] += NT
            dve.wait_ge(s_rt, count[0])
            link(dve.tensor_copy(i8f[:, :, :], i8[:, :, :]))
            four = [P, NT, TOP_K, E]
            hot = one_hot[:, 0:NT * TOP_K * E].rearrange("p (t k e) -> p t k e", k=TOP_K, e=E)
            link(dve.tensor_tensor(hot, small[:, 0:E].unsqueeze(1).unsqueeze(1).to_broadcast(four),
                                   i8f[:, :, 0:TOP_K].unsqueeze(3).to_broadcast(four), ALU.is_equal))
            comb3 = comb.rearrange("p (t e) -> p t e", e=E)
            link(dve.tensor_reduce(comb3, hot.rearrange("p t k e -> p t e k"), AX.X, ALU.add))
            link(dve.tensor_tensor(comb, comb, sc, ALU.mult))
            link(dve.tensor_reduce(csum[:, :], comb3, AX.X, ALU.add))
            link(dve.tensor_scalar(csum[:, :], csum[:, :], 1e-20, None, ALU.add))
            link(dve.reciprocal(cs2[:, :], csum[:, :]))
            link(dve.tensor_tensor(comb3, comb3, cs2[:, :].unsqueeze(2).to_broadcast([P, NT, E]), ALU.mult))
            link(dve.tensor_scalar(comb, comb, ROUTE_SCALE, None, ALU.mult))
            cres3 = cres.rearrange("p (t e) -> p t e", e=E)
            link(dve.tensor_copy(cpart[:, :, 0, :], comb3))
            link(dve.tensor_tensor(cres3, comb3, cpart[:, :, 0, :], ALU.subtract))
            link(dve.tensor_copy(cpart[:, :, 1, :], cres3))
            dve.tensor_tensor(cpart[:, :, 2, :], cres3, cpart[:, :, 1, :], ALU.subtract).then_inc(s_cp, 1)

            def second_norm(n):
                dve.wait_ge(s_t4, n + 1)
                for t in range(4 * n, 4 * n + 4):
                    y = yy[:, n % 4, t % 4, :]
                    dve.tensor_tensor(y, bank(6 + n % 2, P, t % 4 * P),
                                      x1[:, t, :], ALU.add).then_inc(s_r, 1)
                dve.wait_ge(s_r, NT + 4 * (n + 1))
                for t in range(4 * n, 4 * n + 4):
                    dve.bn_stats(stats[:, t, :], yy[:, n % 4, t % 4, :]).then_inc(s_bn, 1)
                dve.wait_ge(s_bn, NT + 4 * (n + 1))
                for t in range(4 * n, 4 * n + 4):
                    dve.bn_aggr(mv[:, t, :], stats[:, t, :]).then_inc(s_mv, 1)
                dve.wait_ge(s_mv, NT + 4 * (n + 1))
                dve.tensor_scalar(ve[:, 4 * n:4 * n + 4], mv[:, 4 * n:4 * n + 4, 1], EPS, None,
                                  ALU.add).then_inc(s_ve, 1)
                dve.wait_ge(s_rs, n + 2)
                for t in range(4 * n, 4 * n + 4):
                    y = yy[:, n % 4, t % 4, :]
                    dve.tensor_scalar(y, y, mv[:, t, 0:1], rstd[:, t:t + 1], ALU.subtract, ALU.mult).then_inc(s_y, 1)

            for n in range(NC):
                for u in range(NU):
                    i = NU * n + u
                    dve.wait_ge(s_sg, i + 1)
                    if u < NPAIR:
                        if i >= 2:
                            dve.wait_ge(s_hh, i - 1)
                        dve.wait_ge(s_u, i + 1)
                        dve.tensor_tensor(au[:, i % 2, :], bank(2 + i % 2), sg[:, i % 2, :], ALU.mult).then_inc(s_au, 1)
                        dve.wait_ge(s_au, pairs(i + 1))
                        dve.wait_ge(s_cb, NPAIR * n + u + 1)
                        if i >= 2:
                            dve.wait_ge(s_dn, i - 1)
                        dve.tensor_tensor(hh[:, i % 2, :], bank(4 + i % 2), au[:, i % 2, :], ALU.mult).then_inc(s_hh, 1)
                    else:
                        dve.wait_ge(s_u, i + 1)
                        dve.wait_ge(s_dn, i - 1)
                        dve.tensor_tensor(hh[:, i % 2, :], bank(2 + i % 2), sg[:, i % 2, :], ALU.mult).then_inc(s_hh, 1)
                    if n >= 1 and u == 6:
                        second_norm(n - 1)
            second_norm(NC - 1)

        @block.tensor
        def _(pe):
            pe.wait_ge(s_w, 80)
            for n in range(2 * NC):
                if n % 2 == 0:
                    pe.wait_ge(s_xt[n // 2], 16)
                if n >= 2:
                    pe.wait_ge(s_q32, 2 * (n - 1))
                n4 = n // 2
                pe.matmul(bank(n % 2), (wq, wk)[n % 2][:, :], xT[:, n4 * BANK:(n4 + 1) * BANK],
                          start=True, stop=True).then_inc(s_pj, 1)
            pe.wait_ge(s_c, 16 * 6)
            for n in range(NC):
                if n >= 2:
                    pe.wait_ge(s_v, n - 1)
                for t in range(4):
                    tt = 4 * n + t
                    mm = pe.matmul(bank(2 + n % 2, P, t * P), xT[:, tt * P:(tt + 1) * P], wv[:, :],
                                   start=True, stop=True)
                mm.then_inc(s_vp, 1)

            def max_unit(g, n):
                s = g % NS
                if n == 0:
                    pe.wait_ge(s_rows[s], 96 * (g // NS + 1))
                if n >= 2:
                    pe.wait_ge(s_mxd, (NM - 1) * g + n - 1)
                elif g >= 1 and n == 1:
                    pe.wait_ge(s_mxd, (NM - 1) * g)
                elif g >= 1:
                    pe.wait_ge(s_mc, 3 * g - 1)
                if n == NM - 1:
                    pe.wait_ge(s_mxc, g + 1)
                    pe.transpose(bank(6, P)[0:HG * KT, :], mx[:, 0, :, :].rearrange("p j q -> p (j q)"),
                                 ident[:, :]).then_inc(s_sm, 1)
                    return
                cells, _, part = MAXU[n]
                for j, qt, k0, m, at in cells:
                    q = rows_q[0:K_MAX, s, j * T + qt * P:j * T + (qt + 1) * P]
                    mm = pe.matmul(bank(6 + n % 2, m, at), q, rows_k[0:K_MAX, s, j * T + k0:j * T + k0 + m],
                                   start=True, stop=part == 1)
                    if part == 0:
                        mm = pe.matmul(bank(6 + n % 2, P, at), identb[:, :], mask_qk[:, :], start=False, stop=True)
                mm.then_inc(s_sm, 1)

            def exp_unit(g, n):
                s = g % NS
                kt, j0, per, stride = EXPU[n]
                if n == 0:
                    pe.wait_ge(s_rows[s], 96 * (g // NS + 1))
                    pe.wait_ge(s_mrow[s], 48 * (g // NS + 1))
                if NE * g + n >= 2:
                    pe.wait_ge(s_ex, NE * g + n - 1)
                cols = P * (kt + 1)
                for a_ in range(per):
                    j = j0 + a_
                    base = (n % 2) * 2 * BANK + a_ * stride
                    k = rows_k[0:K_EXP, s, j * T + kt * P:j * T + (kt + 1) * P]
                    for c0 in range(0, cols, BANK):
                        m = min(BANK, cols - c0)
                        last = c0 + m == cols
                        mm = pe.matmul(ps[:, base + c0:base + c0 + m], k, rows_q[0:K_EXP, s, j * T + c0:j * T + c0 + m],
                                       start=True, stop=not last)
                        if last:
                            mm = pe.matmul(ps[:, base + cols - P:base + cols], identb[:, :], mask_kq[:, :],
                                           start=False, stop=True)
                mm.then_inc(s_st, 1)

            def values(g, kt):
                if kt == KT - 1:
                    pe.wait_ge(s_vg, g + 1)
                    if g >= 1:
                        pe.wait_ge(s_ea, g)
                pe.wait_ge(s_ex, NE * g + EXPS_UP_TO[kt])
                cols = P * (kt + 1)
                for c0 in range(0, cols, BANK):
                    m = min(BANK, cols - c0)
                    for j in range(HG):
                        mm = pe.matmul(ps[STRIP * j:STRIP * (j + 1), 4 * BANK + c0:4 * BANK + c0 + m],
                                       Vg[:, g % 2, kt, j, :], probs[:, (KT - 1 - kt) % 2, j * T + c0:j * T + c0 + m],
                                       start=kt == KT - 1, stop=kt == 0 or (c0 > 0 and kt == BANK // P),
                                       tile_position=(0, STRIP * j), skip_group_check=True)
                mm.then_inc(s_pv, 1)

            def steps():
                todo = []
                for n, (kt, j, per, _) in enumerate(EXPU):
                    if (j == 0 or per == HG) and kt + 2 < KT:
                        todo.append(("v", kt + 2, 4 * P * (kt + 3)))
                    todo.append(("e", n, per * P * (kt + 2)))
                return todo + [("v", 1, 8 * P), ("v", 0, 4 * P)]

            STEPS = steps()
            whole = sum(c for _, _, c in STEPS)
            for n in range(NM):
                max_unit(0, n)
            for g in range(NG):
                spent = at = 0
                for kind, n, cost in STEPS:
                    if kind == "e":
                        exp_unit(g, n)
                    else:
                        values(g, n)
                    spent += cost
                    while g + 1 < NG and at < NM and at * whole < spent * NM:
                        max_unit(g + 1, at)
                        at += 1
                while g + 1 < NG and at < NM:
                    max_unit(g + 1, at)
                    at += 1

            def by_token(t):
                b, tt = t // KT, t % KT
                if t == 0:
                    pe.wait_ge(s_ea, NG)
                    pe.wait_ge(s_mxd, (NM - 1) * NG)
                if t >= 2:
                    pe.wait_ge(s_at, t - 1)
                for g in range(GPB):
                    mm = pe.transpose(bank(t % 2, P, g * P), oT[:, b * GPB + g, tt * P:(tt + 1) * P], ident[:, :])
                mm.then_inc(s_t1, 1)

            def by_channel(t):
                pe.wait_ge(s_at, t + 1)
                if t >= 2:
                    pe.wait_ge(s_aT, t - 1)
                pe.transpose(bank(2 + t % 2, P), att[:, t % 2, :], ident[:, :]).then_inc(s_t2, 1)

            def project(t):
                pe.wait_ge(s_aT, t + 1)
                if t >= 2:
                    pe.wait_ge(s_r, t - 1)
                pe.matmul(bank(4 + t % 2, P), attT[:, t % 2, :], wo[:, :], start=True, stop=True).then_inc(s_wo, 1)

            for t in range(NT + 2):
                if t < NT:
                    by_token(t)
                if 1 <= t <= NT:
                    by_channel(t - 1)
                if t >= 2:
                    project(t - 2)
            for n in range(NC):
                pe.wait_ge(s_x1, 4 * (n + 1))
                if n >= 2:
                    pe.wait_ge(s_lo, n - 1)
                for t in range(4):
                    mm = pe.transpose(bank(6 + n % 2, P, t * P), x1[:, 4 * n + t, :], ident[:, :])
                mm.then_inc(s_t3, 1)
            pe.wait_ge(s_gl, 2)
            pe.wait_ge(s_lo, NC)
            for t in range(NT):
                cut = slice(t * P, (t + 1) * P)
                o = bank(0, E, t * E)
                pe.matmul(o, x1hi[:, cut], gate_hi[:, :], start=True, stop=False)
                pe.matmul(o, x1hi[:, cut], gate_lo[:, :], start=False, stop=False)
                mm = pe.matmul(o, x1lo[:, cut], gate_hi[:, :], start=False, stop=True)
            mm.then_inc(s_lg, 1)
            pe.wait_ge(s_cp, 1)
            for c in range(2):
                for t in range(KT):
                    o = bank(2 + c).bitcast(bf16)[0:3 * E, t * P:(t + 1) * P]
                    mm = pe.transpose(o, cpart[:, c * KT + t, :, :].rearrange("p h e -> p (h e)"), identb[:, :])
                mm.then_inc(s_ct, 1)

            def up(n, u):
                i = NU * n + u
                cut = slice(n * BANK, (n + 1) * BANK)
                for half_, dst, ready in ((0, bank(i % 2), s_g), (1, bank(2 + i % 2), s_u)):
                    if i >= 2 and half_ == 0:
                        pe.wait_ge(s_sg, i - 1)
                    if i >= 2 and half_ == 1:
                        wait_read(pe, i - 2)
                    w = slice(half_ * P, (half_ + 1) * P)
                    pe.matmul(dst, gu_hi[:, u, w], x1hi[:, cut], start=True, stop=False)
                    pe.matmul(dst, gu_hi[:, u, w], x1lo[:, cut], start=False, stop=False)
                    pe.matmul(dst, gu_lo[:, u, w], x1hi[:, cut], start=False, stop=True).then_inc(ready, 1)
                if u < NPAIR:
                    if i >= 2:
                        pe.wait_ge(s_hh, i - 1)
                    pe.matmul(bank(4 + i % 2), sel[:, u * P:(u + 1) * P], combT[:, cut],
                              start=True, stop=True).then_inc(s_cb, 1)

            def down_unit(n, u):
                i = NU * n + u
                pe.wait_ge(s_hh, i + 1)
                if u == 0 and n >= 2:
                    pe.wait_ge(s_r, NT + 4 * (n - 1))
                mm = pe.matmul(bank(6 + n % 2), down[:, u, :], hh[:, i % 2, :], start=u == 0, stop=u == NU - 1)
                mm.then_inc(s_dn, 1)

            def back(n):
                pe.wait_ge(s_mo, n + 1)
                for t in range(4):
                    mm = pe.transpose(bank(6 + n % 2, P, t * P), moT[:, n % 2, t * P:(t + 1) * P], ident[:, :])
                mm.then_inc(s_t4, 1)

            pe.wait_ge(s_cT, 2)
            pe.wait_ge(s_gs, 2 * NU)
            pe.wait_ge(s_mw, 32)
            for i in range(NC * NU + 1):
                if i < NC * NU:
                    up(i // NU, i % NU)
                if i >= 1:
                    down_unit((i - 1) // NU, (i - 1) % NU)
                if i >= NU and i % NU == 5:
                    back(i // NU - 1)
            back(NC - 1)


def kernel(**inputs):
    import numpy as np
    import ml_dtypes
    import concourse.bacc as bacc
    from concourse import mybir as mb
    from concourse.bass_utils import run_bass_kernel_spmd as run

    v = {k: np.asarray(a) for k, a in inputs.items()}

    def by_depth(w):
        return w.reshape(GPB, HG, D, -1).transpose(0, 2, 1, 3).reshape(C, -1)

    gate_up = v["L0_ffn_experts_gate_up"].reshape(NPAIR, 2, 2, I, C).transpose(4, 0, 2, 1, 3).reshape(C, NPAIR, 2 * P)
    shared = np.concatenate([v["L0_ffn_shared_gate_w"].T, v["L0_ffn_shared_up_w"].T], 1)[:, None, :]
    down = v["L0_ffn_experts_down"].reshape(NPAIR, 2, C, I).transpose(1, 3, 0, 2).reshape(P, NPAIR, C)
    tokens = v["L0_attn_x"].reshape(NTOK, C)
    at = np.arange(P)
    qb, kb = (at // CHUNK * CHUNK)[:, None], (at // CHUNK * CHUNK)[None, :]
    masked = (qb >= kb) & (at[None, :] - at[:, None] - 2 * (kb - qb) >= 1)
    mask = np.where(masked, np.float32(-3e38), np.float32(0)).astype(ml_dtypes.bfloat16)
    e, u, half = np.ogrid[0:3 * E, 0:NPAIR, 0:P]
    order = np.arange(N_GROUP)
    arrays = {
        "x": tokens, "xT": tokens.T,
        "wqT": by_depth(v["L0_attn_Wq"]).T, "wkT": by_depth(v["L0_attn_Wk"]).T,
        "wvT": v["L0_attn_Wv"].T, "woT": v["L0_attn_Wo"].T,
        "bq": by_depth(v["L0_attn_bq"]), "bk": by_depth(v["L0_attn_bk"]),
        "bv": v["L0_attn_bv"][None], "bo": v["L0_attn_bo"][None],
        "attn_scale": v["L0_attn_attn_scale"][None],
        "gateT": v["L0_ffn_gate_weight"].T, "ebias": v["L0_ffn_e_score_correction_bias"][None],
        "guT": np.concatenate([gate_up, shared], 1),
        "downT": np.concatenate([down, v["L0_ffn_shared_down_w"].T[:, None, :]], 1),
        "ident": np.eye(P, dtype=np.float32), "ident_bf16": np.eye(P, dtype=ml_dtypes.bfloat16),
        "mask_qk": mask, "mask_kq": mask.T,
        "sel": (e % E == 2 * u + half // I).reshape(3 * E, NPAIR * P).astype(ml_dtypes.bfloat16),
        "small": np.tile(np.concatenate([np.arange(E), (order[None, :] < order[:, None]).ravel()]
                                        ).astype(np.float32)[None], (P, 1)),
    }
    nc = bacc.Bacc("TRN2", target_bir_lowering=False, num_devices=1)
    feeds, a = {}, {}
    for name, array in arrays.items():
        array = np.ascontiguousarray(array)
        feeds[f"in_{name}"] = array
        a[name] = nc.dram_tensor(f"in_{name}", array.shape, mb.dt.from_np(array.dtype), kind="ExternalInput").ap()
    a["scratch"] = nc.dram_tensor("scratch", (2, B, 3, C, T), mb.dt.bfloat16).ap()
    out = nc.dram_tensor("out", (NTOK, C), mb.dt.float32, kind="ExternalOutput").ap()
    build(nc, a, out)
    r = run(nc, [feeds], core_ids=[0])
    return r.results[0]["out"].reshape(B, T, C)
```

```python
import concourse.bass as bass
from concourse import mybir
from concourse.alu_op_type import AluOpType as ALU
from contextlib import ExitStack

P = 128
B, T, C = 2, 1024, 128
HEADS, D = 16, 8
CHUNK = 64
E, I, TOP_K = 32, 64, 6
N_GROUP, TOPK_GROUP = 8, 4
ROUTE_SCALE = 2.5
EPS = 1e-5
BANK = 512

NTOK = B * T
NT = NTOK // P
NC = NTOK // BANK
KT = T // P
HG = 4
GPB = HEADS // HG
NG = B * GPB
STRIP = P // HG
NS = 3
NPAIR = E // 2
WIDE_G = N_GROUP + 8 - TOPK_GROUP
WIDE_E = E + 8 - TOP_K
NU = NPAIR + 1

ROWS_QK = 48
MROW = 96
K_MAX = 72
K_EXP = MROW + 3


ONES = float.fromhex("0x1.007f000000000p+0")


def max_units():
    units = []
    for qt in range(KT - 1, -1, -1):
        n = T - P * qt
        for part, (k0, m) in enumerate([(P * qt, min(n, BANK)), (P * qt + BANK, n - BANK)]):
            if m <= 0:
                continue
            per = BANK // m if BANK % m == 0 else 1
            for j in range(0, HG, per):
                units.append(([(j + a, qt, k0, m, a * m) for a in range(per)], m, part))
    return units


def exp_units():
    units = []
    for kt in range(KT - 1, -1, -1):
        n = P * (kt + 1)
        if n > BANK:
            per, stride = 1, 2 * BANK
        elif 2 * n > BANK:
            per, stride = 2, BANK
        else:
            per, stride = 4, n
        units += [(kt, j, per, stride) for j in range(0, HG, per)]
    return units


MAXU, EXPU = max_units(), exp_units()
NM = len(MAXU) + 1
NE = len(EXPU)
EXPS_UP_TO = {kt: sum(u[0] >= kt for u in EXPU) for kt in range(KT)}
PIECE = 256
PIECES = [(kt, c0) for kt in range(KT - 1, -1, -1) for c0 in range(0, P * (kt + 1), PIECE)]
NV = len(PIECES)
PIECES_UP_TO = {kt: sum(p[0] >= kt for p in PIECES) for kt in range(KT)}
UPPER_DONE = PIECES_UP_TO[KT // 2]

QUAD = 4
TAIL = ([("out", 0, t) for t in range(QUAD)] + [("turn", 0, 0), ("proj", 0, 0)]
        + [("out", 1, t) for t in range(QUAD)] + [("turn", 1, 0), ("x1T", 0, 0), ("proj", 1, 0), ("logit", 0, 0),
                                                  ("x1T", 1, 0), ("logit", 1, 0), ("comb", 0, 0), ("comb", 1, 0)])
TAIL_AT = dict(zip([*range(14), 18, 20, 30, 31], range(len(TAIL))))
NORM_AT = (7, 14)
ROUTER_AT, ROUTER_SLICES = 21, 8
LAST = -3e38


def attention_order():
    ev, mm, vv = ([(g, n) for g in range(NG) for n in range(k)] for k in (NE, NM, NV))
    hop, rows_latency, load = 240, 4500, 6000
    LEAD = 1.5
    t = act = dve = tail_ready = 0.0
    e_done, x_done, m_done, v_done = {}, {}, {}, {}
    copied = {(-1, 0): 0.0, (-1, 1): 0.0}
    act_todo, pe_order, act_order, masks_before = [], [], [], []
    tt = [(0, n) for n in range(len(TAIL))]
    i = {"e": 0, "m": 0, "v": 0, "t": 0}
    lag = {"out": 800, "turn": 900, "proj": 1100, "x1T": 1500, "logit": 700, "comb": 0}
    streams = {"e": ev, "m": mm, "v": vv, "t": tt}

    def run_act(until):
        nonlocal act
        while act_todo:
            what, g, n, ready, cost = min(act_todo, key=lambda a: max(a[3], act))
            start = max(ready, act)
            if start > until:
                return
            act_todo.remove((what, g, n, ready, cost))
            act = start + cost
            act_order.append((what, g, n))
            {"x": x_done, "c": copied, "t": {}}[what][g, n] = act + hop

    def ready_e():
        k = i["e"]
        g, n = ev[k]
        kt = EXPU[n][0]
        out = max(m_done.get((g, NM - 1), 1e18) + rows_latency, x_done.get(ev[k - 2], 1e18) if k >= 2 else 0)
        order = KT * g + KT - 1 - kt
        if order >= 2:
            pg, pk = (order - 2) // KT, KT - 1 - (order - 2) % KT
            out = max(out, v_done.get((pg, PIECES_UP_TO[pk] - 1), 1e18) - 300)
        return out

    def ready_m():
        k = i["m"]
        g, n = mm[k]
        if k / NM - i["e"] / NE > LEAD and i["e"] < len(ev):
            return 1e18
        out = m_done.get(mm[k - 2], 1e18) if k >= 2 else 0
        if n == NM - 1:
            out = max(out, m_done[g, n - 1] + 5 * hop)
        if g >= NS:
            out = max(out, e_done.get((g - NS, NE - 1), 1e18) + load)
        return out

    def ready_v():
        g, n = vv[i["v"]]
        kt, c0 = PIECES[n]
        out = x_done.get((g, EXPS_UP_TO[kt] - 1), 1e18) + (1200 if n + 1 == PIECES_UP_TO[kt] else 0)
        if kt == KT - 1:
            out = max(out, copied.get((g - 1, c0 // BANK), 1e18))
        return out

    def ready_t():
        return tail_ready if i["m"] == len(mm) else 1e18

    while any(i[k] < len(s) for k, s in streams.items()):
        run_act(t)
        ready = [(f(), rank, k) for rank, (k, f, s) in enumerate(
            (("t", ready_t, tt), ("m", ready_m, mm), ("e", ready_e, ev), ("v", ready_v, vv))) if i[k] < len(s)]
        now = [c for c in ready if c[0] <= t]
        if not now and act_todo and min(c[0] for c in ready) > min(max(a[3], act) for a in act_todo):
            run_act(min(max(a[3], act) for a in act_todo))
            continue
        when, _, k = min(now, key=lambda c: c[1]) if now else min(ready)
        t = max(t, when)
        if k == "e":
            g, n = ev[i[k]]
            kt, _, per, _ = EXPU[n]
            t += per * P * (kt + 2) / 2.4
            e_done[g, n] = t
            act_todo.append(("x", g, n, t + hop, per * P * (kt + 1) / 1.2 + 130))
        elif k == "m":
            g, n = mm[i[k]]
            if n < NM - 1:
                cells, m, part = MAXU[n]
                t += len(cells) * (m + P * (part == 0)) / 2.4
                dve = max(dve, t + hop) + len(cells) * m / 0.96 + 70
            else:
                t += P / 2.4
                dve = max(dve, t + hop) + 1000
            m_done[g, n] = dve
            tail_ready = dve
        elif k == "t":
            kind, q, _ = TAIL[i[k]]
            if kind == "x1T":
                masks_before.append(sum(x_done.get((g, EXPS_UP_TO[kt] - 1), 1e18) <= t - 1500
                                        for g in range(NG) for kt in range(KT)))
            t += {"proj": 900, "logit": 400, "comb": 250}.get(kind, 250)
            tail_ready = t + lag[kind]
            if kind == "proj":
                x1_ready = t + 3500
            if i[k] + 1 < len(TAIL) and TAIL[i[k] + 1][0] == "x1T":
                tail_ready = max(tail_ready, x1_ready)
            if kind == "logit" and TAIL[i[k] + 1][0] == "comb":
                tail_ready = t + 14000
            if kind in ("turn", "x1T", "logit", "comb"):
                act_todo.append(("t", 0, i[k], t + hop, 500))
        else:
            g, n = vv[i[k]]
            kt, c0 = PIECES[n]
            t += 4 * min(PIECE, P * (kt + 1) - c0) / 2.4 + 70
            v_done[g, n] = t
            if n == UPPER_DONE - 1:
                act_todo.append(("c", g, 1, t + hop, 560))
            elif n == NV - 1:
                act_todo.append(("c", g, 0, t + hop, 560))
        pe_order.append((k, *streams[k][i[k]]))
        i[k] += 1
    run_act(1e18)
    return pe_order, act_order, masks_before, t


def build(nc, a, out):
    f32, bf16, f32r = mybir.dt.float32, mybir.dt.bfloat16, mybir.dt.float32r
    u32 = mybir.dt.uint32
    ACT, AX = mybir.ActivationFunctionType, mybir.AxisListType
    ctx = ExitStack()
    with ctx:
        def sb(name, shape, dt):
            return ctx.enter_context(nc.sbuf_tensor(name, shape, dt))

        def sem(name):
            return ctx.enter_context(nc.semaphore(name))

        ident = sb("ident", [P, P], f32)
        identb = sb("identb", [P, P], bf16)
        mask_qk = sb("mask_qk", [P, P], bf16)
        wo = sb("wo", [P, C], f32)
        bq, bk, bqs = (sb(n, [P, 1], f32) for n in ("bq", "bk", "bqs"))
        scale = sb("scale", [P, 1], f32)
        ones = sb("ones", [1, P], f32)
        bob, ebias = sb("bob", [P, C], f32), sb("ebias", [P, E], f32)
        gate_w = sb("gate_w", [P, E], f32)
        gate_hi, gate_lo = sb("gate_hi", [P, E], f32r), sb("gate_lo", [P, E], f32r)
        w_raw = sb("w_raw", [P, 2, 3 * P], f32)
        w_hi, w_lo = (sb(n, [P, NU, 3 * P], f32r) for n in ("w_hi", "w_lo"))
        x = sb("x", [P, NT, C], f32)
        Vg = sb("Vg", [P, 2, KT, HG, STRIP], f32)
        rows_q = sb("rows_q", [P, NS, HG * T], bf16)
        rows_k = sb("rows_k", [P, NS, HG * T], bf16)
        mx = sb("mx", [P, 2, HG, KT], f32)
        mh = sb("mh", [HG * KT, 3, P], bf16)
        mr = sb("mr", [HG * KT, P], f32)
        oT = sb("oT", [P, NG, T], f32)
        rec = sb("rec", [P, 2, HEADS], f32)
        stats = sb("stats", [P, NT, 6], f32)
        mv = sb("mv", [P, NT, 2], f32)
        ve, half, rstd = (sb(n, [P, NT], f32) for n in ("ve", "half", "rstd"))
        csum, cs2 = sb("csum", [P, KT], f32), sb("cs2", [P, KT], f32)
        with ExitStack() as early:
            def first(name, shape, dt):
                return early.enter_context(nc.sbuf_tensor(name, shape, dt))

            xT, V = first("xT", [P, NTOK], f32), first("V", [P, NT, C], f32)
            wq, wk, wv, bvr = (first(n, [P, C], f32) for n in ("wq", "wk", "wv", "bvr"))
            spare = first("spare", [P, 4 * C], f32)
            probs = first("probs", [P, 2, HG * T], f32)
        x1hi, x1lo = (sb(n, [P, NTOK], f32r) for n in ("x1hi", "x1lo"))
        att, attT = (sb(n, [P, QUAD * C], f32) for n in ("att", "attT"))
        sg, au, hh, moT = (sb(n, [P, 2, BANK], f32) for n in ("sg", "au", "hh", "moT"))
        hhi, hlo = (sb(n, [P, 2, BANK], f32r) for n in ("hhi", "hlo"))
        yy = sb("yy", [P, 2, QUAD, C], f32)
        q32 = oT[:, 0, :].rearrange("p (s n) -> p s n", s=2)
        r32 = oT[:, 1, :].rearrange("p (s n) -> p s n", s=2)
        parts = oT[:, 2:8, :].rearrange("p a b -> p (a b)").bitcast(bf16).rearrange("p (s h n) -> p s h n", h=3, n=BANK)
        work = oT[:, 0:GPB, :].rearrange("p a b -> p (a b)")
        at = [0]

        def piece_of(n):
            at[0] += n
            return work[:, at[0] - n:at[0]]

        sc, sfc, comb, ex = (piece_of(KT * E) for _ in range(4))
        comb3 = comb.rearrange("p (t e) -> p t e", e=E)
        gs, g_rest = (piece_of(KT * WIDE_G).rearrange("p (t g) -> p t g", g=WIDE_G) for _ in range(2))
        msk, rest = (piece_of(KT * WIDE_E).rearrange("p (t e) -> p t e", e=WIDE_E) for _ in range(2))
        keep = piece_of(KT * N_GROUP).rearrange("p (t g) -> p t g", g=N_GROUP)
        g8, m8 = (piece_of(KT * 8).rearrange("p (t k) -> p t k", k=8) for _ in range(2))
        combT = rows_q[0:E, NS - 1, :].bitcast(f32)
        comb_rows = rows_k[:, NS - 1, :].bitcast(f32).rearrange("p (s t) -> p s t", t=BANK)
        CB = HG * T // 2 // BANK

        ps = ctx.enter_context(nc.psum_tensor("ps", [P, 8 * BANK], f32))

        def bank(n, cols=BANK, at=0):
            return ps[:, n * BANK + at:n * BANK + at + cols]

        s_wq = sem("s_wq")
        s_w = sem("s_w")
        s_xt = [sem(f"s_xt{n}") for n in range(NC)]
        s_one = sem("s_one")
        s_c = sem("s_c")
        s_c2 = sem("s_c2")
        s_cw = [sem(f"s_cw{n}") for n in range(NC)]
        s_cb = [sem(f"s_cb{n}") for n in range(CB)]
        s_gw = [sem("s_gw0"), sem("s_gw1")]
        s_bqs = sem("s_bqs")
        s_pj = sem("s_pj")
        s_q32 = sem("s_q32")
        s_split = sem("s_split")
        s_parts = sem("s_parts")
        s_scr = [sem("s_scr0"), sem("s_scr1")]
        s_vp = sem("s_vp")
        s_v = sem("s_v")
        s_zero0 = sem("s_zero0")
        s_zero = sem("s_zero")
        s_rows = [sem(f"s_rows{n}") for n in range(NS)]
        s_mrow = [sem(f"s_mrow{n}") for n in range(NS)]
        s_sm = sem("s_sm")
        s_mxd = sem("s_mxd")
        s_mxc = sem("s_mxc")
        s_mc = sem("s_mc")
        s_mh = sem("s_mh")
        s_st = sem("s_st")
        s_ex = sem("s_ex")
        s_vg = sem("s_vg")
        s_pv = sem("s_pv")
        s_ea = [sem("s_ea0"), sem("s_ea1")]
        s_gs = sem("s_gs")
        s_t1, s_rc, s_at, s_t2, s_aT, s_wo = (sem(n) for n in ("s_t1", "s_rc", "s_at", "s_t2", "s_aT", "s_wo"))
        s_r, s_bn, s_mv, s_ve, s_rs, s_hf, s_x1 = (sem(n) for n in ("s_r", "s_bn", "s_mv", "s_ve", "s_rs", "s_hf", "s_x1"))
        s_t3, s_hi, s_lo, s_lg, s_sig, s_rt, s_cp, s_ct, s_cT = (
            sem(n) for n in ("s_t3", "s_hi", "s_lo", "s_lg", "s_sig", "s_rt", "s_cp", "s_ct", "s_cT"))
        s_g, s_u, s_sg, s_au, s_hh, s_hhi, s_hlo, s_dn, s_mo, s_t4, s_y4 = (
            sem(n) for n in ("s_g", "s_u", "s_sg", "s_au", "s_hh", "s_hhi", "s_hlo", "s_dn", "s_mo", "s_t4", "s_y4"))
        s_y, s_xb, s_gl, s_mk, s_lk = sem("s_y"), sem("s_xb"), sem("s_gl"), sem("s_mk"), sem("s_lk")
        s_out = [sem("s_out0"), sem("s_out1")]
        s_tc = [sem("s_tc6"), sem("s_tc7")]

        scr = a["scratch"]

        def pairs(i):
            return i - i // NU

        def wait_read(eng, i):
            if i % NU < NPAIR:
                eng.wait_ge(s_au, pairs(i + 1))
            else:
                eng.wait_ge(s_hh, i + 1)

        TOP = 6 + NM % 2
        FIRST_BANKS = (6, 7, 0, 1)

        def max_bank(g, n):
            return FIRST_BANKS[n % len(FIRST_BANKS)] if g == 0 else 6 + n % 2
        ACC, BACK = 6, 7
        BACK_AT = {33: 0, 38: 1, 55: 2}
        SUM_AT = {at + 2: n for at, n in BACK_AT.items()}
        STORE_AT = {at + 9: n for at, n in SUM_AT.items() if n < NC - 2}
        ROOT_AT = {NORM_AT[0] + 1: (2, 2 * QUAD), NORM_AT[1] + 1: (3, 3 * QUAD),
                   **{at + 2: (4 + n, QUAD * n) for at, n in SUM_AT.items()}, NC * NU: (7, 3 * QUAD)}

        def tail_bank(b, k):
            which = k % 2 if b == 0 else 1
            return s_tc[which], bank(6 + which)

        def tail_count(b, k):
            return k // 2 + 1 if b == 0 else len(TAIL) // 2 + k + 1

        def wait_step(eng, b, k):
            eng.wait_ge(tail_bank(b, k)[0], tail_count(b, k))

        pe_order, act_order, masks_before, _ = attention_order()
        block = ctx.enter_context(nc.Block())

        @block.sync
        def _(sp):
            def load_chunk(n):
                sp.dma_start(xT[:, n * BANK:(n + 1) * BANK], a["xT"][:, n * BANK:(n + 1) * BANK]).then_inc(s_xt[n], 16)

            load_chunk(0)
            sp.dma_start(wq[:, :], a["wqT"]).then_inc(s_wq, 16)
            sp.dma_start(bq[:, :], a["bq"]).then_inc(s_w, 16)
            sp.dma_start(scale[:, :], a["attn_scale"].to_broadcast([P, 1])).then_inc(s_w, 16)
            sp.dma_start(wk[:, :], a["wkT"]).then_inc(s_w, 16)
            sp.dma_start(bk[:, :], a["bk"]).then_inc(s_w, 16)
            for n in range(1, NC):
                load_chunk(n)
            sp.dma_start(wv[:, :], a["wvT"]).then_inc(s_c, 16)
            sp.dma_start(bvr[0:1, :], a["bv"]).then_inc(s_c, 16)
            sp.dma_start(identb[:, :], a["ident_bf16"]).then_inc(s_c, 16)
            sp.dma_start(mask_qk[:, :], a["mask_qk"]).then_inc(s_c, 16)
            sp.dma_start(ident[:, :], a["ident"]).then_inc(s_c, 16)
            def load_rows(g):
                if g == GPB:
                    sp.wait_ge(s_scr[1], 16 * NC)
                b, r = g // GPB, slice((g % GPB) * STRIP, (g % GPB + 1) * STRIP)
                s = g % NS
                for which, dst, reps in ((0, rows_q, None), (1, rows_k, 3)):
                    part = scr[which, b, :, r, :].rearrange("h (d j) t -> h d (j t)", d=D)
                    if reps is None:
                        spans = ((0, 24, part), (24, 16, part[0:2]), (40, 8, part[0]))
                    else:
                        spans = ((0, 24, part[0:1].to_broadcast([3, D, HG * T])),
                                 (24, 16, part[1:2].to_broadcast([2, D, HG * T])), (40, 8, part[2]))
                    for at, n, src in spans:
                        sp.dma_start(dst[at:at + n, s, :], src).then_inc(s_rows[s], 16)

            for n in range(2 * NC):
                q_or_k, n4 = n % 2, n // 2
                sp.wait_ge(s_parts, n + 1)
                half_batch = slice((n4 % 2) * BANK, (n4 % 2 + 1) * BANK)
                sp.dma_start(scr[q_or_k, n4 // 2][:, :, half_batch].rearrange("h c t -> c h t"),
                             parts[:, n, :, :]).then_inc(s_scr[n4 // 2], 16)
                if n == NC - 1:
                    sp.wait_ge(s_scr[0], 16 * NC)
                    sp.wait_ge(s_zero0, 3)
                    load_rows(0)
            sp.wait_ge(s_zero, 3 * (NS - 1))
            for g in range(1, NS):
                load_rows(g)
            sp.dma_start(x[:, :, :], a["x"].rearrange("(n p) c -> p n c", p=P)).then_inc(s_c2, 16)
            sp.dma_start(wo[:, :], a["woT"]).then_inc(s_c2, 16)
            sp.dma_start(bob[:, :], a["bo"].to_broadcast([P, C])).then_inc(s_c2, 16)
            sp.dma_start(gate_w[:, :], a["gateT"]).then_inc(s_c2, 16)
            sp.dma_start(ebias[:, :], a["ebias"].to_broadcast([P, E])).then_inc(s_c2, 16)

            def load_unit(u):
                if u >= 2:
                    sp.wait_ge(s_gs, 2 * (u - 1))
                sp.dma_start(w_raw[:, u % 2, :], a["unitT"][:, u, :]).then_inc(s_gw[u % 2], 16)

            def store_max(g):
                s = g % NS
                sp.wait_ge(s_mh, g + 1)
                for h in range(3):
                    sp.dma_start(rows_q[MROW + h:MROW + h + 1, s, :], mh[:, h, :]).then_inc(s_mrow[s], 16)

            def store_output(n):
                sp.wait_ge(s_y, QUAD * (n + 1))
                sp.dma_start(out[n * BANK:(n + 1) * BANK, :].rearrange("(t p) c -> p t c", p=P),
                             yy[:, n % 2, :, :]).then_inc(s_out[n % 2], 16)

            u = 0
            for g in range(NG):
                store_max(g)
                if 1 <= g <= NG - NS:
                    sp.wait_ge(s_st, NE * g)
                    load_rows(g + NS - 1)
                for _ in range(3):
                    if u < NU:
                        load_unit(u)
                        u += 1

            sp.wait_ge(s_st, NE * (NG - 2))
            for n in range(NC):
                sp.wait_ge(s_cw[n], 16)
                for u in range(NPAIR):
                    p, i = NPAIR * n + u, NU * n + u
                    if i in STORE_AT:
                        store_output(STORE_AT[i])
                    if p >= CB:
                        q = p - CB
                        sp.wait_ge(s_hh, q + q // NPAIR + 1)
                    for e in range(2):
                        sp.dma_start(comb_rows[e * I:(e + 1) * I, p % CB, :],
                                     a["weights"][2 * u + e:2 * u + e + 1, n * BANK:(n + 1) * BANK]
                                     .to_broadcast([I, BANK])).then_inc(s_cb[p % CB], 16)
            store_output(NC - 2)
            store_output(NC - 1)
            for s in range(2):
                sp.wait_ge(s_out[s], 16 * NC // 2)

        @block.gpsimd
        def _(pool):
            for s in range(1, NS):
                pool.memset(rows_q[0:MROW, s, :].bitcast(f32), 0.0).then_inc(s_zero, 1)
                pool.memset(rows_k[0:MROW, s, :].bitcast(f32), 0.0).then_inc(s_zero, 1)
                pool.wait_ge(s_zero, 3 * s - 1)
                pool.memset(rows_k[MROW:P, s, :].bitcast(f32), ONES).then_inc(s_zero, 1)
                pool.wait_ge(s_zero, 3 * s)
            pool.memset(half[:, :], -0.5).then_inc(s_hf, 1)
            pool.memset(Vg[:, :, :, :, :], 0.0).then_inc(s_hf, 1)
            pool.wait_ge(s_hf, 2)
            pool.memset(Vg[:, :, :, :, D:D + 1], 1.0).then_inc(s_hf, 1)
            pool.wait_ge(s_hf, 3)

            def values(g):
                pool.wait_ge(s_v, 2 * (g // GPB + 1))
                if g >= 2:
                    pool.wait_ge(s_pv, NV * (g - 1))
                c0 = (g % GPB) * STRIP
                src = V[:, (g // GPB) * KT:(g // GPB + 1) * KT, c0:c0 + STRIP]
                pool.tensor_copy(Vg[:, g % 2, :, :, 0:D],
                                 src.rearrange("p k (j d) -> p k j d", d=D)).then_inc(s_vg, 1)
                pool.wait_ge(s_vg, g + 1)

            def mask(g, kt):
                pool.wait_ge(s_ex, NE * g + EXPS_UP_TO[kt])
                v = probs[:, (KT - 1 - kt) % 2, :].rearrange("p (j t) -> p j t", j=HG)
                first_chunk = v[0:CHUNK, :, kt * P:(kt + 1) * P].rearrange("p j (c t) -> p j c t", c=2)
                second_chunk = v[CHUNK:P, :, kt * P + CHUNK:(kt + 1) * P]
                pool.affine_select(out=first_chunk, in_=first_chunk, compare_op=ALU.is_ge, fill=0.0, base=0,
                                   pattern=[[0, HG], [-2 * P, 2], [1, CHUNK]], channel_multiplier=-1).then_inc(s_mk, 1)
                n = 2 * (KT * g + KT - 1 - kt)
                pool.wait_ge(s_mk, n + 1)
                pool.affine_select(out=second_chunk, in_=second_chunk, compare_op=ALU.is_ge, fill=0.0, base=0,
                                   pattern=[[0, HG], [1, CHUNK]], channel_multiplier=-1).then_inc(s_mk, 1)
                pool.wait_ge(s_mk, n + 2)

            def split_unit(u):
                pool.wait_ge(s_gw[u % 2], 16 * (u // 2 + 1))
                pool.tensor_copy(w_hi[:, u, :], w_raw[:, u % 2, :]).then_inc(s_gs, 1)
                pool.wait_ge(s_gs, 2 * u + 1)
                pool.tensor_tensor(w_lo[:, u, :], w_raw[:, u % 2, :], w_hi[:, u, :], ALU.subtract).then_inc(s_gs, 1)
                pool.wait_ge(s_gs, 2 * u + 2)

            def root(n, at, k):
                pool.wait_ge(s_ve, n + 1)
                pool.tensor_tensor(rstd[:, at:at + k], ve[:, at:at + k], half[:, at:at + k], ALU.pow).then_inc(s_rs, 1)
                pool.wait_ge(s_rs, n + 1)

            values(0)
            pool.wait_ge(s_c2, 16 * 5)
            pool.tensor_tensor(x[:, :, :], x[:, :, :], bob[:, :].unsqueeze(1).to_broadcast([P, NT, C]),
                               ALU.add).then_inc(s_xb, 1)
            pool.wait_ge(s_xb, 1)
            u = 0
            for g in range(NG):
                for kt in range(KT - 1, -1, -1):
                    mask(g, kt)
                    for q in range(2):
                        if KT * g + KT - kt == masks_before[q]:
                            root(q, q * QUAD, QUAD)
                    if kt == KT - 2 and g + 1 < NG:
                        values(g + 1)
                    if kt in (6, 5, 4) and u < NU:
                        split_unit(u)
                        u += 1

            def low_part(i):
                pool.wait_ge(s_hhi, i + 1)
                if i >= 2:
                    pool.wait_ge(s_dn, i - 1)
                pool.tensor_tensor(hlo[:, i % 2, :], hh[:, i % 2, :], hhi[:, i % 2, :], ALU.subtract).then_inc(s_hlo, 1)

            for i in range(NC * NU):
                if i in ROOT_AT:
                    n, at_ = ROOT_AT[i]
                    root(n, at_, QUAD)
                low_part(i)
            root(*ROOT_AT[NC * NU], QUAD)

        @block.scalar
        def _(act):
            act.wait_ge(s_w, 64)
            act.activation(bqs[:, :], bq[:, :], ACT.Copy, scale=scale[:, 0:1]).then_inc(s_bqs, 1)
            act.wait_ge(s_bqs, 1)
            for n in range(2 * NC):
                act.wait_ge(s_pj, n + 1)
                if n >= 2:
                    act.wait_ge(s_parts, n - 1)
                how = dict(scale=scale[:, 0:1], bias=bqs[:, 0:1]) if n % 2 == 0 else dict(bias=bk[:, 0:1])
                act.activation(q32[:, n % 2, :], bank(n % 2), ACT.Identity, **how).then_inc(s_q32, 1)
                act.activation(parts[:, n, 0, :], bank(n % 2), ACT.Identity, **how).then_inc(s_q32, 1)

            for n in range(NC):
                act.wait_ge(s_vp, n + 1)
                act.copy(V[:, 4 * n:4 * n + 4, :], bank(2 + n).rearrange("p (t c) -> p t c", c=C)).then_inc(s_v, 1)

            def exponentials(g, n):
                kt, j, per, stride = EXPU[n]
                cols = P * (kt + 1)
                act.wait_ge(s_st, NE * g + n + 1)
                if KT * g + KT - 1 - kt >= 2:
                    pg, pk = (g, kt + 2) if kt + 2 < KT else (g - 1, kt + 2 - KT)
                    act.wait_ge(s_pv, NV * pg + PIECES_UP_TO[pk])
                src = ps[:, (n % 2) * 2 * BANK:(n % 2 + 1) * 2 * BANK]
                if per > 1:
                    src = src[:, 0:per * stride].rearrange("p (j n) -> p j n", j=per)[:, :, 0:cols]
                    dst = probs[:, (KT - 1 - kt) % 2, :].rearrange("p (j n) -> p j n", j=HG)[:, j:j + per, 0:cols]
                else:
                    src = src[:, 0:cols]
                    dst = probs[:, (KT - 1 - kt) % 2, j * T:j * T + cols]
                act.activation(dst, src, ACT.Exp).then_inc(s_ex, 1)

            def copy_output(g, h):
                act.wait_ge(s_pv, NV * g + (UPPER_DONE if h else NV))
                act.copy(oT[:, g, h * BANK:(h + 1) * BANK], bank(4 + h)).then_inc(s_ea[h], 1)

            def tail_step(b, k):
                kind, q, _ = TAIL[k]
                n, (o, src) = 2 * b + q, tail_bank(b, k)
                if kind == "turn":
                    act.wait_ge(s_t2, n + 1)
                    act.copy(attT[:, :], src).then_inc(o, 1)
                elif kind == "x1T":
                    act.wait_ge(s_t3, n + 1)
                    if n == 0:
                        act.wait_ge(s_vg, NG)
                    act.copy(x1hi[:, n * BANK:(n + 1) * BANK], src).then_inc(s_hi, 1)
                elif kind == "logit":
                    act.wait_ge(s_lg, n + 1)
                    if n == 2:
                        act.wait_ge(s_cp, 1)
                    act.activation(ex[:, q * QUAD * E:(q + 1) * QUAD * E], src[:, 0:QUAD * E], ACT.Exp,
                                   scale=-1.0).then_inc(o, 1)
                elif kind == "comb":
                    act.wait_ge(s_ct, n + 1)
                    cols = slice(n * BANK, (n + 1) * BANK)
                    act.copy(combT[:, cols], src[0:E, :]).then_inc(o, 1)
                    act.wait_ge(o, tail_count(b, k))
                    act.dma_start(a["weights"][:, cols], combT[:, cols]).then_inc(s_cw[n], 16)

            for kind, g, n in act_order:
                if kind == "x":
                    exponentials(g, n)
                elif kind == "c":
                    copy_output(g, n)
                else:
                    tail_step(g, n)

            def expert_sum(n):
                act.wait_ge(s_dn, NU * (n + 1))
                if n >= 2:
                    act.wait_ge(s_t4, n - 1)
                act.copy(moT[:, n % 2, :], bank(ACC)).then_inc(s_mo, 1)

            def high_part(i):
                act.wait_ge(s_hh, i + 1)
                if i >= 2:
                    act.wait_ge(s_dn, i - 1)
                act.copy(hhi[:, i % 2, :], hh[:, i % 2, :]).then_inc(s_hhi, 1)

            for i in range(NC * NU + 1):
                if i >= NU and i % NU == 2:
                    expert_sum(i // NU - 1)
                if i - 1 in TAIL_AT:
                    tail_step(1, TAIL_AT[i - 1])
                if i < NC * NU:
                    act.wait_ge(s_g, i + 1)
                    if i >= 2:
                        wait_read(act, i - 2)
                    act.activation(sg[:, i % 2, :], bank(i % 2), ACT.Silu).then_inc(s_sg, 1)
                if i >= 1:
                    high_part(i - 1)
            expert_sum(NC - 1)

        @block.vector
        def _(dve):
            dve.memset(ones[:, :], 1.0).then_inc(s_one, 1)
            dve.memset(rows_q[0:MROW, 0, :].bitcast(f32), 0.0).then_inc(s_zero0, 1)
            dve.memset(rows_k[0:MROW, 0, :].bitcast(f32), 0.0).then_inc(s_zero0, 1)
            dve.memset(rows_k[MROW:P, 0, :].bitcast(f32), ONES).then_inc(s_zero0, 1)
            for n in range(2 * NC):
                s = n % 2
                dve.wait_ge(s_q32, 2 * n + 2)
                dve.tensor_tensor(r32[:, s, :], q32[:, s, :], parts[:, n, 0, :], ALU.subtract).then_inc(s_split, 1)
                dve.wait_ge(s_split, 2 * n + 1)
                dve.tensor_copy(parts[:, n, 1, :], r32[:, s, :]).then_inc(s_split, 1)
                dve.wait_ge(s_split, 2 * n + 2)
                dve.tensor_tensor(parts[:, n, 2, :], r32[:, s, :], parts[:, n, 1, :], ALU.subtract).then_inc(s_parts, 1)

            def maxima(g):
                for n, (cells, m, part) in enumerate(MAXU):
                    j, qt = cells[0][:2]
                    per = len(cells)
                    dve.wait_ge(s_sm, NM * g + n + 1)
                    src = bank(max_bank(g, n), per * m).rearrange("p (j m) -> p j m", j=per)
                    dve.tensor_reduce(mx[:, part, j:j + per, qt], src, AX.X, ALU.max).then_inc(s_mxd, 1)
                wide = KT - BANK // P
                dve.wait_ge(s_mxd, (NM - 1) * (g + 1))
                dve.tensor_tensor(mx[:, 0, :, 0:wide], mx[:, 0, :, 0:wide], mx[:, 1, :, 0:wide],
                                  ALU.max).then_inc(s_mxc, 1)
                if g >= 1:
                    dve.wait_ge(s_mrow[(g - 1) % NS], 48 * ((g - 1) // NS + 1))
                top = bank(TOP, P)[0:HG * KT, :]
                dve.wait_ge(s_sm, NM * (g + 1))
                dve.tensor_scalar(mh[:, 0, :], top, -1.0, None, ALU.mult).then_inc(s_mc, 1)
                dve.wait_ge(s_mc, 3 * g + 1)
                dve.scalar_tensor_tensor(mr[:, :], top, -1.0, mh[:, 0, :], ALU.mult, ALU.subtract).then_inc(s_mc, 1)
                dve.wait_ge(s_mc, 3 * g + 2)
                dve.tensor_copy(mh[:, 1, :], mr[:, :]).then_inc(s_mc, 1)
                dve.wait_ge(s_mc, 3 * g + 3)
                dve.tensor_tensor(mh[:, 2, :], mr[:, :], mh[:, 1, :], ALU.subtract).then_inc(s_mh, 1)

            for g in range(NG):
                maxima(g)

            dve.wait_ge(s_c2, 16 * 5)
            dve.tensor_copy(gate_hi[:, :], gate_w[:, :]).then_inc(s_gl, 1)
            dve.wait_ge(s_gl, 1)
            dve.tensor_tensor(gate_lo[:, :], gate_w[:, :], gate_hi[:, :], ALU.subtract).then_inc(s_gl, 1)
            dve.wait_ge(s_xb, 1)

            count = [0]

            def link(*steps):
                if count[0]:
                    dve.wait_ge(s_lk, count[0])
                for step in steps:
                    step().then_inc(s_lk, 1)
                count[0] += len(steps)

            def output(b, k):
                _, q, i = TAIL[k]
                t, (done, src) = KT * b + QUAD * q + i, tail_bank(b, k)
                o = src.rearrange("p (h e) -> p h e", e=STRIP)
                dve.wait_ge(s_t1, t + 1)
                dve.reciprocal(rec[:, t % 2, :], o[:, :, D]).then_inc(s_rc, 1)
                dve.wait_ge(s_rc, t + 1)
                if i == 0 and t:
                    dve.wait_ge(s_t2, 2 * b + q)
                if t == 0:
                    dve.wait_ge(s_v, NC)
                dve.tensor_tensor(att[:, i * C:(i + 1) * C].rearrange("p (h d) -> p h d", d=D), o[:, :, 0:D],
                                  rec[:, t % 2, :].unsqueeze(2).to_broadcast([P, HEADS, D]),
                                  ALU.mult).then_inc(done, 1)

            def residual(b, k):
                n, (done, src) = 2 * b + TAIL[k][1], tail_bank(b, k)
                dve.wait_ge(s_wo, n + 1)
                quad = x[:, QUAD * n:QUAD * (n + 1), :]
                dve.tensor_tensor(quad, src.rearrange("p (t c) -> p t c", c=C), quad, ALU.add).then_inc(done, 1)

            def statistics(b, k):
                n, (done, _) = 2 * b + TAIL[k][1], tail_bank(b, k)
                dve.wait_ge(done, tail_count(b, k))
                for t in range(QUAD * n, QUAD * (n + 1)):
                    dve.bn_stats(stats[:, t, :], x[:, t, :]).then_inc(s_bn, 1)

            def aggregate(n, before):
                dve.wait_ge(s_bn, before + QUAD)
                for t in range(QUAD * n, QUAD * (n + 1)):
                    dve.bn_aggr(mv[:, t, :], stats[:, t, :]).then_inc(s_mv, 1)
                dve.wait_ge(s_mv, before + QUAD)
                quad = slice(QUAD * n, QUAD * (n + 1))
                dve.tensor_scalar(ve[:, quad], mv[:, quad, 1], EPS, None, ALU.add).then_inc(s_ve, 1)

            def first_norm(n, before):
                dve.wait_ge(s_rs, before + 1)
                for t in range(QUAD * n, QUAD * (n + 1)):
                    dve.tensor_scalar(x[:, t, :], x[:, t, :], mv[:, t, 0:1], rstd[:, t:t + 1],
                                      ALU.subtract, ALU.mult).then_inc(s_x1, 1)

            def x1_low(b, k):
                n, (done, src) = 2 * b + TAIL[k][1], tail_bank(b, k)
                dve.wait_ge(s_hi, n + 1)
                cols = slice(n * BANK, (n + 1) * BANK)
                dve.tensor_tensor(x1lo[:, cols], src, x1hi[:, cols], ALU.subtract).then_inc(done, 1)

            sc3, sfc3 = (v.rearrange("p (t e) -> p t e", e=E) for v in (sc, sfc))
            per = E // N_GROUP
            by_token = [P, KT, E]

            def router(b, n):
                if n == 0:
                    for q in range(2):
                        k = TAIL.index(("logit", q, 0))
                        dve.wait_ge(tail_bank(b, k)[0], tail_count(b, k))
                    link(lambda: dve.tensor_scalar(ex, ex, 1.0, None, ALU.add))
                    link(lambda: dve.reciprocal(sc, ex))
                    if b == 0:
                        link(lambda: dve.memset(gs[:, :, N_GROUP:], LAST))
                        link(lambda: dve.memset(msk[:, :, E:], LAST))
                elif n == 1:
                    link(lambda: dve.tensor_tensor(sfc3, sc3, ebias[:, :].unsqueeze(1).to_broadcast(by_token), ALU.add))
                    link(lambda: dve.tensor_reduce(gs[:, :, 0:N_GROUP], sfc.rearrange("p (t g e) -> p t g e", e=per, g=N_GROUP),
                                                   AX.X, ALU.max))
                elif n == 2:
                    link(*(lambda t=t: dve.max(g8[:, t, :], gs[:, t, 0:N_GROUP]) for t in range(KT)))
                elif n == 3:
                    link(lambda: dve.memset(g8[:, :, TOPK_GROUP:], LAST))
                    link(*(lambda t=t: dve.match_replace(g_rest[:, t, :], g8[:, t, :], gs[:, t, :], LAST) for t in range(KT)))
                    link(lambda: dve.tensor_tensor(keep, gs[:, :, 0:N_GROUP], g_rest[:, :, 0:N_GROUP], ALU.not_equal))
                    link(lambda: dve.tensor_tensor(
                        msk[:, :, 0:E].rearrange("p t (g e) -> p t g e", e=per),
                        sfc.rearrange("p (t g e) -> p t g e", e=per, g=N_GROUP),
                        keep.unsqueeze(3).to_broadcast([P, KT, N_GROUP, per]), ALU.mult))
                elif n == 4:
                    link(*(lambda t=t: dve.max(m8[:, t, :], msk[:, t, 0:E]) for t in range(KT)))
                elif n == 5:
                    link(lambda: dve.memset(m8[:, :, TOP_K:], LAST))
                    link(*(lambda t=t: dve.match_replace(rest[:, t, :], m8[:, t, :], msk[:, t, :], LAST) for t in range(KT)))
                elif n == 6:
                    if b:
                        dve.wait_ge(s_ct, 2)
                    link(lambda: dve.tensor_tensor(comb3, msk[:, :, 0:E], rest[:, :, 0:E], ALU.not_equal))
                    link(lambda: dve.tensor_tensor(comb, comb, sc, ALU.mult))
                elif n == 7:
                    link(lambda: dve.tensor_reduce(csum[:, :], comb3, AX.X, ALU.add))
                    link(lambda: dve.tensor_scalar(csum[:, :], csum[:, :], 1e-20, None, ALU.add))
                    link(lambda: dve.reciprocal(cs2[:, :], csum[:, :]))
                    dve.wait_ge(s_lk, count[0])
                    dve.scalar_tensor_tensor(comb3, comb3, ROUTE_SCALE, cs2[:, :].unsqueeze(2).to_broadcast(by_token),
                                             ALU.mult, ALU.mult).then_inc(s_cp, 1)

            def tail(b, at):
                k = TAIL_AT.get(at - 1)
                if k is not None and TAIL[k][0] == "out":
                    output(b, k)
                elif k is not None and TAIL[k][0] == "proj":
                    residual(b, k)
                elif k is not None and TAIL[k][0] == "x1T":
                    x1_low(b, k)
                for q, first_at in enumerate(NORM_AT):
                    p = TAIL.index(("proj", q, 0))
                    n = 2 * b + q
                    if at == first_at:
                        statistics(b, p)
                    elif at == first_at + 1:
                        aggregate(n, QUAD * n)
                    elif at == first_at + 3:
                        first_norm(n, n)
                if ROUTER_AT <= at < ROUTER_AT + ROUTER_SLICES:
                    router(b, at - ROUTER_AT)

            for at_ in range(ROUTER_AT + ROUTER_SLICES):
                tail(0, at_)

            def second_sum(n):
                dve.wait_ge(s_t4, n + 1)
                if n >= 2:
                    dve.wait_ge(s_out[n % 2], 16 * (n // 2))
                dve.tensor_tensor(yy[:, n % 2, :, :], bank(BACK).rearrange("p (t c) -> p t c", c=C),
                                  x[:, QUAD * n:QUAD * (n + 1), :], ALU.add).then_inc(s_y4, 1)

            def second_norm(n, step):
                if step == 0:
                    second_sum(n)
                elif step == 1:
                    dve.wait_ge(s_y4, n + 1)
                    for t in range(QUAD * n, QUAD * (n + 1)):
                        dve.bn_stats(stats[:, t, :], yy[:, n % 2, t % QUAD, :]).then_inc(s_bn, 1)
                elif step == 2:
                    aggregate(n, QUAD * (4 + n))
                else:
                    dve.wait_ge(s_rs, (4 + n) + 1)
                    for t in range(QUAD * n, QUAD * (n + 1)):
                        y = yy[:, n % 2, t % QUAD, :]
                        dve.tensor_scalar(y, y, mv[:, t, 0:1], rstd[:, t:t + 1], ALU.subtract, ALU.mult).then_inc(s_y, 1)

            for i in range(NC * NU):
                n, u = i // NU, i % NU
                if i < ROUTER_AT + ROUTER_SLICES:
                    tail(1, i)
                for first_at, m in SUM_AT.items():
                    if i - first_at in (0, 1, 2, 4):
                        second_norm(m, i - first_at)
                dve.wait_ge(s_sg, i + 1)
                dve.wait_ge(s_u, i + 1)
                if i >= 2:
                    dve.wait_ge(s_hlo, i - 1)
                if u < NPAIR:
                    dve.tensor_tensor(au[:, i % 2, :], bank(2 + i % 2), sg[:, i % 2, :], ALU.mult).then_inc(s_au, 1)
                    dve.wait_ge(s_au, pairs(i + 1))
                    p = NPAIR * n + u
                    dve.wait_ge(s_cb[p % CB], 32 * (p // CB + 1))
                    dve.tensor_tensor(hh[:, i % 2, :], comb_rows[:, p % CB, :], au[:, i % 2, :], ALU.mult).then_inc(s_hh, 1)
                else:
                    dve.tensor_tensor(hh[:, i % 2, :], bank(2 + i % 2), sg[:, i % 2, :], ALU.mult).then_inc(s_hh, 1)
            for step in (0, 1, 2, 4):
                second_norm(NC - 1, step)

        @block.tensor
        def _(pe):
            pe.wait_ge(s_wq, 16)
            for n in range(2 * NC):
                if n == 1:
                    pe.wait_ge(s_w, 64)
                if n % 2 == 0:
                    pe.wait_ge(s_xt[n // 2], 16)
                if n >= 2:
                    pe.wait_ge(s_q32, 2 * (n - 1))
                n4 = n // 2
                pe.matmul(bank(n % 2), (wq, wk)[n % 2][:, :], xT[:, n4 * BANK:(n4 + 1) * BANK],
                          start=True, stop=True).then_inc(s_pj, 1)
            pe.wait_ge(s_c, 16 * 5)
            pe.wait_ge(s_one, 1)
            for n in range(NC):
                for t in range(4):
                    tt = 4 * n + t
                    pe.matmul(bank(2 + n, P, t * P), xT[:, tt * P:(tt + 1) * P], wv[:, :],
                              start=True, stop=False)
                    mm = pe.matmul(bank(2 + n, P, t * P), ones[0:1, :], bvr[0:1, :], start=False, stop=True)
                mm.then_inc(s_vp, 1)

            def max_unit(g, n):
                s = g % NS
                if n == 0:
                    pe.wait_ge(s_rows[s], 96 * (g // NS + 1))
                if g == 0 and n == 2:
                    pe.wait_ge(s_q32, 4 * NC)
                turn = len(FIRST_BANKS) if g == 0 else 2
                if n >= turn and n < NM - 1:
                    pe.wait_ge(s_mxd, (NM - 1) * g + n + 1 - turn)
                elif g >= 1 and n == 0:
                    pe.wait_ge(s_mxd, (NM - 1) * g)
                elif g >= 1:
                    pe.wait_ge(s_mc, 3 * g - 1)
                if n == NM - 1:
                    pe.wait_ge(s_mxc, g + 1)
                    pe.transpose(bank(TOP, P)[0:HG * KT, :], mx[:, 0, :, :].rearrange("p j q -> p (j q)"),
                                 ident[:, :]).then_inc(s_sm, 1)
                    return
                cells, _, part = MAXU[n]
                for j, qt, k0, m, at in cells:
                    q = rows_q[0:K_MAX, s, j * T + qt * P:j * T + (qt + 1) * P]
                    mm = pe.matmul(bank(max_bank(g, n), m, at), q, rows_k[0:K_MAX, s, j * T + k0:j * T + k0 + m],
                                   start=True, stop=part == 1)
                    if part == 0:
                        mm = pe.matmul(bank(max_bank(g, n), P, at), identb[:, :], mask_qk[:, :], start=False, stop=True)
                mm.then_inc(s_sm, 1)

            def exp_unit(g, n):
                s = g % NS
                kt, j0, per, stride = EXPU[n]
                if n == 0:
                    pe.wait_ge(s_rows[s], 96 * (g // NS + 1))
                    pe.wait_ge(s_mrow[s], 48 * (g // NS + 1))
                if g == 0 and n == 1:
                    pe.wait_ge(s_v, NC)
                if NE * g + n >= 2:
                    pe.wait_ge(s_ex, NE * g + n - 1)
                cols = P * (kt + 1)
                for a_ in range(per):
                    j = j0 + a_
                    base = (n % 2) * 2 * BANK + a_ * stride
                    k = rows_k[0:K_EXP, s, j * T + kt * P:j * T + (kt + 1) * P]
                    for c0 in range(0, cols, BANK):
                        m = min(BANK, cols - c0)
                        mm = pe.matmul(ps[:, base + c0:base + c0 + m], k, rows_q[0:K_EXP, s, j * T + c0:j * T + c0 + m],
                                       start=True, stop=True)
                mm.then_inc(s_st, 1)

            def values(g, n):
                kt, c0 = PIECES[n]
                if kt == KT - 1:
                    pe.wait_ge(s_vg, g + 1)
                    if g >= 1:
                        pe.wait_ge(s_ea[c0 // BANK], g)
                pe.wait_ge(s_ex, NE * g + EXPS_UP_TO[kt])
                if n + 1 == PIECES_UP_TO[kt]:
                    pe.wait_ge(s_mk, 2 * (KT * g + KT - kt))
                m = min(PIECE, P * (kt + 1) - c0)
                for j in range(HG):
                    mm = pe.matmul(ps[STRIP * j:STRIP * (j + 1), 4 * BANK + c0:4 * BANK + c0 + m],
                                   Vg[:, g % 2, kt, j, :], probs[:, (KT - 1 - kt) % 2, j * T + c0:j * T + c0 + m],
                                   start=kt == KT - 1 and c0 % BANK == 0, stop=n + 1 in (UPPER_DONE, NV),
                                   tile_position=(0, STRIP * j), skip_group_check=True)
                mm.then_inc(s_pv, 1)

            def tail_step(b, k):
                kind, q, i = TAIL[k]
                n, (done, dst) = 2 * b + q, tail_bank(b, k)
                if b == 0 and k < 2:
                    pe.wait_ge(*((s_mxd, (NM - 1) * NG) if k == 0 else (s_mc, 3 * NG - 1)))
                else:
                    pe.wait_ge(done, tail_count(b, k) - 1)
                if kind == "out":
                    if q == 0 and i == 0:
                        for h in range(2):
                            pe.wait_ge(s_ea[h], GPB * (b + 1))
                    t = QUAD * q + i
                    for g in range(GPB):
                        mm = pe.transpose(dst[:, g * P:(g + 1) * P], oT[:, b * GPB + g, t * P:(t + 1) * P], ident[:, :])
                    mm.then_inc(s_t1, 1)
                elif kind == "turn":
                    last = TAIL.index(("out", q, QUAD - 1))
                    wait_step(pe, b, last)
                    wait_step(pe, b, last - 1)
                    for t in range(QUAD):
                        mm = pe.transpose(dst[:, t * P:(t + 1) * P], att[:, t * C:(t + 1) * C], ident[:, :])
                    mm.then_inc(s_t2, 1)
                elif kind == "proj":
                    wait_step(pe, b, TAIL.index(("turn", q, 0)))
                    for t in range(QUAD):
                        mm = pe.matmul(dst[:, t * P:(t + 1) * P], attT[:, t * P:(t + 1) * P], wo[:, :],
                                       start=True, stop=True)
                    mm.then_inc(s_wo, 1)
                elif kind == "x1T":
                    pe.wait_ge(s_x1, QUAD * (n + 1))
                    for t in range(QUAD):
                        mm = pe.transpose(dst[:, t * P:(t + 1) * P], x[:, QUAD * n + t, :], ident[:, :])
                    mm.then_inc(s_t3, 1)
                elif kind == "logit":
                    wait_step(pe, b, TAIL.index(("x1T", q, 0)))
                    pe.wait_ge(s_gl, 2)
                    for t in range(QUAD):
                        cols = slice((QUAD * n + t) * P, (QUAD * n + t + 1) * P)
                        o = dst[:, t * E:(t + 1) * E]
                        pe.matmul(o, x1hi[:, cols], gate_hi[:, :], start=True, stop=False)
                        pe.matmul(o, x1hi[:, cols], gate_lo[:, :], start=False, stop=False)
                        mm = pe.matmul(o, x1lo[:, cols], gate_hi[:, :], start=False, stop=True)
                    mm.then_inc(s_lg, 1)
                else:
                    pe.wait_ge(s_cp, b + 1)
                    for t in range(QUAD):
                        mm = pe.transpose(dst[0:E, t * P:(t + 1) * P], comb3[:, QUAD * q + t, :], ident[:, :])
                    mm.then_inc(s_ct, 1)

            def up(i):
                n, u = i // NU, i % NU
                cols = slice(n * BANK, (n + 1) * BANK)
                for half_, dst, ready in ((0, bank(i % 2), s_g), (1, bank(2 + i % 2), s_u)):
                    if i >= 2 and half_ == 0:
                        pe.wait_ge(s_sg, i - 1)
                    if i >= 2 and half_ == 1:
                        wait_read(pe, i - 2)
                    w = slice(half_ * P, (half_ + 1) * P)
                    pe.matmul(dst, w_hi[:, u, w], x1hi[:, cols], start=True, stop=False)
                    pe.matmul(dst, w_hi[:, u, w], x1lo[:, cols], start=False, stop=False)
                    pe.matmul(dst, w_lo[:, u, w], x1hi[:, cols], start=False, stop=True).then_inc(ready, 1)

            for kind, g, n in pe_order:
                if kind == "e":
                    exp_unit(g, n)
                elif kind == "m":
                    max_unit(g, n)
                elif kind == "v":
                    i = n - (NV - 2)
                    if g == NG - 1 and i in (0, 1):
                        if i == 0:
                            pe.wait_ge(s_gs, 2 * NU)
                            pe.wait_ge(s_ex, NE * NG)
                        up(i)
                    values(g, n)
                else:
                    tail_step(g, n)

            def down(i):
                n, u = i // NU, i % NU
                pe.wait_ge(s_hlo, i + 1)
                if u == 0 and n >= 1:
                    pe.wait_ge(s_mo, n)
                w = slice(2 * P, 3 * P)
                pe.matmul(bank(ACC), w_hi[:, u, w], hhi[:, i % 2, :], start=u == 0, stop=False)
                pe.matmul(bank(ACC), w_lo[:, u, w], hhi[:, i % 2, :], start=False, stop=False)
                pe.matmul(bank(ACC), w_hi[:, u, w], hlo[:, i % 2, :], start=False, stop=u == NU - 1).then_inc(s_dn, 1)

            def back(n):
                pe.wait_ge(s_mo, n + 1)
                if n == 0:
                    wait_step(pe, 1, TAIL.index(("comb", 1, 0)))
                else:
                    pe.wait_ge(s_y4, n)
                for t in range(QUAD):
                    mm = pe.transpose(bank(BACK, P, t * P), moT[:, n % 2, t * P:(t + 1) * P], ident[:, :])
                mm.then_inc(s_t4, 1)

            for h in range(2):
                pe.wait_ge(s_ea[h], NG)
            for i in range(NC * NU + 2):
                if 2 <= i < NC * NU:
                    up(i)
                if i in BACK_AT:
                    back(BACK_AT[i])
                if i >= 2:
                    down(i - 2)
                if i in TAIL_AT:
                    tail_step(1, TAIL_AT[i])
            back(NC - 1)


def kernel(**inputs):
    import numpy as np
    import ml_dtypes
    import concourse.bacc as bacc
    from concourse import mybir as mb
    from concourse.bass_utils import run_bass_kernel_spmd as run

    v = {k: np.asarray(a) for k, a in inputs.items()}

    def by_depth(w):
        return w.reshape(GPB, HG, D, -1).transpose(0, 2, 1, 3).reshape(C, -1)

    gate_up = v["L0_ffn_experts_gate_up"].reshape(NPAIR, 2, 2, I, C).transpose(4, 0, 2, 1, 3).reshape(C, NPAIR, 2 * P)
    shared = np.concatenate([v["L0_ffn_shared_gate_w"].T, v["L0_ffn_shared_up_w"].T], 1)[:, None, :]
    down = v["L0_ffn_experts_down"].reshape(NPAIR, 2, C, I).transpose(1, 3, 0, 2).reshape(P, NPAIR, C)
    tokens = v["L0_attn_x"].reshape(NTOK, C)
    at = np.arange(P)
    qb, kb = (at // CHUNK * CHUNK)[:, None], (at // CHUNK * CHUNK)[None, :]
    masked = (qb >= kb) & (at[None, :] - at[:, None] - 2 * (kb - qb) >= 1)
    mask = np.where(masked, np.float32(-3e38), np.float32(0)).astype(ml_dtypes.bfloat16)
    arrays = {
        "x": tokens, "xT": tokens.T,
        "wqT": by_depth(v["L0_attn_Wq"]).T, "wkT": by_depth(v["L0_attn_Wk"]).T,
        "wvT": v["L0_attn_Wv"].T, "woT": v["L0_attn_Wo"].T,
        "bq": by_depth(v["L0_attn_bq"]), "bk": by_depth(v["L0_attn_bk"]),
        "bv": v["L0_attn_bv"][None], "bo": v["L0_attn_bo"][None],
        "attn_scale": v["L0_attn_attn_scale"][None],
        "gateT": v["L0_ffn_gate_weight"].T, "ebias": v["L0_ffn_e_score_correction_bias"][None],
        "unitT": np.concatenate([np.concatenate([gate_up, shared], 1),
                                 np.concatenate([down, v["L0_ffn_shared_down_w"].T[:, None, :]], 1)], 2),
        "ident": np.eye(P, dtype=np.float32), "ident_bf16": np.eye(P, dtype=ml_dtypes.bfloat16),
        "mask_qk": mask,
    }
    nc = bacc.Bacc("TRN2", target_bir_lowering=False, num_devices=1)
    feeds, a = {}, {}
    for name, array in arrays.items():
        array = np.ascontiguousarray(array)
        feeds[f"in_{name}"] = array
        a[name] = nc.dram_tensor(f"in_{name}", array.shape, mb.dt.from_np(array.dtype), kind="ExternalInput").ap()
    a["scratch"] = nc.dram_tensor("scratch", (2, B, 3, C, T), mb.dt.bfloat16).ap()
    a["weights"] = nc.dram_tensor("weights", (E, NTOK), mb.dt.float32).ap()
    out = nc.dram_tensor("out", (NTOK, C), mb.dt.float32, kind="ExternalOutput").ap()
    build(nc, a, out)
    r = run(nc, [feeds], core_ids=[0])
    return r.results[0]["out"].reshape(B, T, C)
```

```python
import concourse.bass as bass
from concourse import mybir
from concourse.alu_op_type import AluOpType as ALU
from contextlib import ExitStack

P = 128
B, T, C = 2, 1024, 128
HEADS, D = 16, 8
CHUNK = 64
E, I, TOP_K = 32, 64, 6
N_GROUP, TOPK_GROUP = 8, 4
ROUTE_SCALE = 2.5
EPS = 1e-5
BANK = 512

NTOK = B * T
NT = NTOK // P
NC = NTOK // BANK
KT = T // P
HG = 4
GPB = HEADS // HG
NG = B * GPB
STRIP = P // HG
NS = 3
NPAIR = E // 2
WIDE_G = N_GROUP + 8 - TOPK_GROUP
WIDE_E = E + 8 - TOP_K
NU = NPAIR + 1

ROWS_QK = 48
MROW = 96
K_MAX = 72
K_EXP = MROW + 3


ONES = float.fromhex("0x1.007f000000000p+0")


def max_units():
    units = []
    for qt in range(KT - 1, -1, -1):
        n = T - P * qt
        for part, (k0, m) in enumerate([(P * qt, min(n, BANK)), (P * qt + BANK, n - BANK)]):
            if m <= 0:
                continue
            per = BANK // m if BANK % m == 0 else 1
            for j in range(0, HG, per):
                units.append(([(j + a, qt, k0, m, a * m) for a in range(per)], m, part))
    return units


def exp_units():
    units = []
    for kt in range(KT - 1, -1, -1):
        n = P * (kt + 1)
        if n > BANK:
            per, stride = 1, 2 * BANK
        elif 2 * n > BANK:
            per, stride = 2, BANK
        else:
            per, stride = 4, n
        units += [(kt, j, per, stride) for j in range(0, HG, per)]
    return units


MAXU, EXPU = max_units(), exp_units()
NM = len(MAXU) + 1
NE = len(EXPU)
EXPS_UP_TO = {kt: sum(u[0] >= kt for u in EXPU) for kt in range(KT)}
PIECE = 256
PIECES = [(kt, c0) for kt in range(KT - 1, -1, -1) for c0 in range(0, P * (kt + 1), PIECE)]
NV = len(PIECES)
PIECES_UP_TO = {kt: sum(p[0] >= kt for p in PIECES) for kt in range(KT)}
UPPER_DONE = PIECES_UP_TO[KT // 2]

HALF = KT // 2
PLACE = {kt: ((KT - 1 - kt) % 2, 0) if kt >= HALF else ((HALF - 1 - kt) // 2, (HALF - 1 - kt) % 2 * BANK)
         for kt in range(KT)}
PLACE_FROM = {kt: (0, kt + 2) if kt >= HALF else (0, HALF + 1 - PLACE[kt][0]) for kt in range(KT - 2)}
PLACE_FROM.update({KT - 1: (-1, HALF - 2), KT - 2: (-1, 0)})

QUAD = 4
TAIL = ([("out", 0, t) for t in range(QUAD)] + [("turn", 0, 0), ("proj", 0, 0)]
        + [("out", 1, t) for t in range(QUAD)] + [("turn", 1, 0), ("x1T", 0, 0), ("proj", 1, 0), ("logit", 0, 0),
                                                  ("x1T", 1, 0), ("logit", 1, 0), ("comb", 0, 0), ("comb", 1, 0)])
COMB = TAIL.index(("comb", 0, 0))
TAIL_AT = dict(zip([*range(1, 15), 19, 21, 31, 32], range(len(TAIL))))
NORM_AT = (8, 15)
ROUTER_AT, ROUTER_SLICES = 22, 8
LAST = -3e38


def attention_order():
    ev, mm, vv = ([(g, n) for g in range(NG) for n in range(k)] for k in (NE, NM, NV))
    hop, rows_latency, load = 240, 5500, 6000
    LEAD = 1.5
    t = act = dve = tail_ready = 0.0
    e_done, x_done, m_done, v_done = {}, {}, {}, {}
    copied = {(-1, 0): 0.0, (-1, 1): 0.0}
    act_todo, pe_order, act_order, masks_before = [], [], [], []
    tt = [(0, n) for n in range(COMB)]
    i = {"e": 0, "m": 0, "v": 0, "t": 0}
    lag = {"out": 800, "turn": 900, "proj": 1100, "x1T": 1500, "logit": 700, "comb": 0}
    streams = {"e": ev, "m": mm, "v": vv, "t": tt}

    def run_act(until):
        nonlocal act
        while act_todo:
            what, g, n, ready, cost = min(act_todo, key=lambda a: max(a[3], act))
            start = max(ready, act)
            if start > until:
                return
            act_todo.remove((what, g, n, ready, cost))
            act = start + cost
            act_order.append((what, g, n))
            {"x": x_done, "c": copied, "t": {}}[what][g, n] = act + hop

    def ready_e():
        k = i["e"]
        g, n = ev[k]
        kt = EXPU[n][0]
        out = max(m_done.get((g, NM - 1), 1e18) + rows_latency, x_done.get(ev[k - 2], 1e18) if k >= 2 else 0)
        pg, pk = PLACE_FROM[kt]
        if g + pg >= 0:
            pg += g
            out = max(out, v_done.get((pg, PIECES_UP_TO[pk] - 1), 1e18) - 300)
        return out

    def ready_m():
        k = i["m"]
        g, n = mm[k]
        if k / NM - i["e"] / NE > LEAD and i["e"] < len(ev):
            return 1e18
        out = m_done.get(mm[k - 2], 1e18) if k >= 2 else 0
        if n == NM - 1:
            out = max(out, m_done[g, n - 1] + 2 * hop)
        if g >= NS:
            out = max(out, e_done.get((g - NS, NE - 1), 1e18) + load)
        return out

    def ready_v():
        g, n = vv[i["v"]]
        kt, c0 = PIECES[n]
        out = x_done.get((g, EXPS_UP_TO[kt] - 1), 1e18) + (1200 if n + 1 == PIECES_UP_TO[kt] else 0)
        if kt == KT - 1:
            out = max(out, copied.get((g - 1, c0 // BANK), 1e18))
        return out

    def ready_t():
        return tail_ready if i["m"] == len(mm) else 1e18

    while any(i[k] < len(s) for k, s in streams.items()):
        run_act(t)
        ready = [(f(), rank, k) for rank, (k, f, s) in enumerate(
            (("t", ready_t, tt), ("m", ready_m, mm), ("e", ready_e, ev), ("v", ready_v, vv))) if i[k] < len(s)]
        now = [c for c in ready if c[0] <= t]
        if not now and act_todo and min(c[0] for c in ready) > min(max(a[3], act) for a in act_todo):
            run_act(min(max(a[3], act) for a in act_todo))
            continue
        when, _, k = min(now, key=lambda c: c[1]) if now else min(ready)
        t = max(t, when)
        if k == "e":
            g, n = ev[i[k]]
            kt, _, per, _ = EXPU[n]
            t += per * P * (kt + 2) / 2.4
            e_done[g, n] = t
            act_todo.append(("x", g, n, t + hop, per * P * (kt + 1) / 1.2 + 130))
        elif k == "m":
            g, n = mm[i[k]]
            if n < NM - 1:
                cells, m, part = MAXU[n]
                t += len(cells) * (m + P * (part == 0)) / 2.4
                dve = max(dve, t + hop) + len(cells) * m / 0.96 + 70
            else:
                t += P / 2.4
                dve = max(dve, t + hop) + 1000
            m_done[g, n] = dve
            tail_ready = dve
        elif k == "t":
            kind, q, _ = TAIL[i[k]]
            if kind == "x1T":
                masks_before.append(sum(x_done.get((g, EXPS_UP_TO[kt] - 1), 1e18) <= t - 1500
                                        for g in range(NG) for kt in range(KT)))
            t += {"proj": 900, "logit": 400, "comb": 250}.get(kind, 250)
            tail_ready = t + lag[kind]
            if kind == "proj":
                x1_ready = t + 3500
            if TAIL[i[k] + 1][0] == "x1T":
                tail_ready = max(tail_ready, x1_ready)
            if kind in ("turn", "x1T", "logit", "comb"):
                act_todo.append(("t", 0, i[k], t + hop, 500))
        else:
            g, n = vv[i[k]]
            kt, c0 = PIECES[n]
            t += 4 * min(PIECE, P * (kt + 1) - c0) / 2.4 + 70
            v_done[g, n] = t
            if n == UPPER_DONE - 1:
                act_todo.append(("c", g, 1, t + hop, 560))
            elif n == NV - 1:
                act_todo.append(("c", g, 0, t + hop, 560))
        pe_order.append((k, *streams[k][i[k]]))
        i[k] += 1
    run_act(1e18)
    return pe_order, act_order, masks_before, t


def build(nc, a, out):
    f32, bf16, f32r = mybir.dt.float32, mybir.dt.bfloat16, mybir.dt.float32r
    ACT, AX = mybir.ActivationFunctionType, mybir.AxisListType
    ctx = ExitStack()
    with ctx:
        def sb(name, shape, dt):
            return ctx.enter_context(nc.sbuf_tensor(name, shape, dt))

        def sem(name):
            return ctx.enter_context(nc.semaphore(name))

        ident = sb("ident", [P, P], f32)
        identb = sb("identb", [P, P], bf16)
        mask_qk = sb("mask_qk", [P, P], bf16)
        wo = sb("wo", [P, C], f32)
        bq, bk, bqs = (sb(n, [P, 1], f32) for n in ("bq", "bk", "bqs"))
        scale = sb("scale", [P, 1], f32)
        ones = sb("ones", [1, P], f32)
        bob, ebias = sb("bob", [P, C], f32), sb("ebias", [P, E], f32)
        gate_w = sb("gate_w", [P, E], f32)
        gate_hi, gate_lo = sb("gate_hi", [P, E], f32r), sb("gate_lo", [P, E], f32r)
        w_raw = sb("w_raw", [P, 2, 3 * P], f32)
        w_hi, w_lo = (sb(n, [P, NU, 3 * P], f32r) for n in ("w_hi", "w_lo"))
        x = sb("x", [P, NT, C], f32)
        Vg = sb("Vg", [P, 2, KT, HG, STRIP], f32)
        rows_q = sb("rows_q", [P, NS, HG * T], bf16)
        rows_k = sb("rows_k", [P, NS, HG * T], bf16)
        mx = sb("mx", [P, 2, HG, KT], f32)
        mh = sb("mh", [HG * KT, 3, P], bf16)
        mr = sb("mr", [HG * KT, P], f32)
        oT = sb("oT", [P, NG, T], f32)
        rec = sb("rec", [P, 2, HEADS], f32)
        stats = sb("stats", [P, NT, 6], f32)
        mv = sb("mv", [P, NT, 2], f32)
        ve, half, rstd = (sb(n, [P, NT], f32) for n in ("ve", "half", "rstd"))
        csum, cs2 = sb("csum", [P, KT], f32), sb("cs2", [P, KT], f32)
        with ExitStack() as early:
            def first(name, shape, dt):
                return early.enter_context(nc.sbuf_tensor(name, shape, dt))

            xT, V = first("xT", [P, NTOK], f32), first("V", [P, NT, C], f32)
            wq, wk, wv, bvr = (first(n, [P, C], f32) for n in ("wq", "wk", "wv", "bvr"))
            first("filler", [P, 4 * C], f32)
            probs = first("probs", [P, 2, HG * T], f32)
        x1hi, x1lo = (sb(n, [P, NTOK], f32r) for n in ("x1hi", "x1lo"))
        att, attT = (sb(n, [P, QUAD * C], f32) for n in ("att", "attT"))
        sg, au, hh, moT = (sb(n, [P, 2, BANK], f32) for n in ("sg", "au", "hh", "moT"))
        hhi, hlo = (sb(n, [P, 2, BANK], f32r) for n in ("hhi", "hlo"))
        yy = sb("yy", [P, 2, QUAD, C], f32)
        q32 = oT[:, 0, :].rearrange("p (s n) -> p s n", s=2)
        r32 = oT[:, 1, :].rearrange("p (s n) -> p s n", s=2)
        parts = oT[:, 2:8, :].rearrange("p a b -> p (a b)").bitcast(bf16).rearrange("p (s h n) -> p s h n", h=3,
                                                                                    n=BANK)
        work = oT[:, 0:GPB, :].rearrange("p a b -> p (a b)")
        at = [0]

        def piece_of(n):
            at[0] += n
            return work[:, at[0] - n:at[0]]

        sc, sfc, comb, ex = (piece_of(KT * E) for _ in range(4))
        comb3 = comb.rearrange("p (t e) -> p t e", e=E)
        gs, g_rest = (piece_of(KT * WIDE_G).rearrange("p (t g) -> p t g", g=WIDE_G) for _ in range(2))
        msk, rest = (piece_of(KT * WIDE_E).rearrange("p (t e) -> p t e", e=WIDE_E) for _ in range(2))
        keep = piece_of(KT * N_GROUP).rearrange("p (t g) -> p t g", g=N_GROUP)
        g8, m8 = (piece_of(KT * 8).rearrange("p (t k) -> p t k", k=8) for _ in range(2))
        combT = rows_q[0:E, NS - 1, :].bitcast(f32)
        comb_rows = rows_k[:, NS - 1, :].bitcast(f32).rearrange("p (s t) -> p s t", t=BANK)
        CB = HG * T // 2 // BANK

        ps = ctx.enter_context(nc.psum_tensor("ps", [P, 8 * BANK], f32))

        def bank(n, cols=BANK, at=0):
            return ps[:, n * BANK + at:n * BANK + at + cols]

        wq_loaded = sem("wq_loaded")
        proj_loaded = sem("proj_loaded")
        xT_loaded = [sem(f"xT_loaded_{n}") for n in range(NC)]
        ones_set = sem("ones_set")
        attn_consts_loaded = sem("attn_consts_loaded")
        tail_consts_loaded = sem("tail_consts_loaded")
        comb_stored = [sem(f"comb_stored_{n}") for n in range(NC)]
        comb_rows_loaded = [sem(f"comb_rows_loaded_{n}") for n in range(CB)]
        unit_loaded = [sem("unit_loaded_0"), sem("unit_loaded_1")]
        bq_scaled = sem("bq_scaled")
        proj_done = sem("proj_done")
        proj_copied = sem("proj_copied")
        split_steps = sem("split_steps")
        parts_ready = sem("parts_ready")
        parts_stored = [sem("parts_stored_0"), sem("parts_stored_1")]
        v_projected = sem("v_projected")
        v_ready = sem("v_ready")
        slot0_cleared = sem("slot0_cleared")
        slots_cleared = sem("slots_cleared")
        rows_loaded = [sem(f"rows_loaded_{n}") for n in range(NS)]
        max_rows_loaded = [sem(f"max_rows_loaded_{n}") for n in range(NS)]
        max_scores = sem("max_scores")
        max_read = sem("max_read")
        max_joined = sem("max_joined")
        max_split_steps = sem("max_split_steps")
        max_split = sem("max_split")
        exp_scores = sem("exp_scores")
        exps_ready = sem("exps_ready")
        values_ready = sem("values_ready")
        values_used = sem("values_used")
        output_copied = [sem("output_copied_0"), sem("output_copied_1")]
        unit_split_steps = sem("unit_split_steps")
        out_by_token = sem("out_by_token")
        sums_inverted = sem("sums_inverted")
        out_by_channel = sem("out_by_channel")
        projected = sem("projected")
        x_biased = sem("x_biased")
        consts_set = sem("consts_set")
        stats_ready = sem("stats_ready")
        moments_ready = sem("moments_ready")
        var_ready = sem("var_ready")
        rstd_ready = sem("rstd_ready")
        x1_normed = sem("x1_normed")
        x1_by_channel = sem("x1_by_channel")
        x1_high = sem("x1_high")
        gate_split = sem("gate_split")
        first_exps = sem("first_exps")
        logits_ready = sem("logits_ready")
        router_steps = sem("router_steps")
        comb_ready = sem("comb_ready")
        comb_by_expert = sem("comb_by_expert")
        gates_ready, ups_ready = sem("gates_ready"), sem("ups_ready")
        silu_ready = sem("silu_ready")
        gated_ready = sem("gated_ready")
        hidden_ready = sem("hidden_ready")
        hidden_high = sem("hidden_high")
        hidden_low = sem("hidden_low")
        down_done = sem("down_done")
        sum_copied = sem("sum_copied")
        sum_by_token = sem("sum_by_token")
        y_summed = sem("y_summed")
        y_ready = sem("y_ready")
        squares_masked = sem("squares_masked")
        out_stored = [sem("out_stored_0"), sem("out_stored_1")]
        tail_read = [sem("tail_read_6"), sem("tail_read_7")]

        scr = a["scratch"]

        def pairs(i):
            return i - (i + NU - 1) // NU

        def wait_read(eng, i):
            if i % NU:
                eng.wait_ge(gated_ready, pairs(i + 1))
            else:
                eng.wait_ge(hidden_ready, i + 1)

        TOP = 6 + NM % 2
        FIRST_BANKS = (6, 7, 0, 1)

        def max_bank(g, n):
            return FIRST_BANKS[n % len(FIRST_BANKS)] if g == 0 else 6 + n % 2
        ACC, BACK = 6, 7
        BACK_AT = {34: 0, 39: 1, 55: 2}
        SUM_AT = {at + 2: n for at, n in BACK_AT.items()}
        STORE_AT = {at + 9: n for at, n in SUM_AT.items() if n < NC - 2}
        ROOT_AT = {NORM_AT[0] + 1: (2, 2 * QUAD), NORM_AT[1] + 1: (3, 3 * QUAD),
                   **{at + 2: (4 + n, QUAD * n) for at, n in SUM_AT.items()}, NC * NU: (7, 3 * QUAD)}

        def tail_bank(b, k):
            which = k % 2 if b == 0 else 1
            return tail_read[which], bank(6 + which)

        def tail_count(b, k):
            return k // 2 + 1 if b == 0 else len(TAIL) // 2 + k + 1

        def wait_step(eng, b, k):
            eng.wait_ge(tail_bank(b, k)[0], tail_count(b, k))

        pe_order, act_order, masks_before, _ = attention_order()
        block = ctx.enter_context(nc.Block())

        @block.sync
        def _(sp):
            def load_chunk(n):
                sp.dma_start(xT[:, n * BANK:(n + 1) * BANK],
                             a["xT"][:, n * BANK:(n + 1) * BANK]).then_inc(xT_loaded[n], 16)

            load_chunk(0)
            sp.dma_start(wq[:, :], a["wqT"]).then_inc(wq_loaded, 16)
            sp.dma_start(bq[:, :], a["bq"]).then_inc(proj_loaded, 16)
            sp.dma_start(scale[:, :], a["attn_scale"].to_broadcast([P, 1])).then_inc(proj_loaded, 16)
            sp.dma_start(wk[:, :], a["wkT"]).then_inc(proj_loaded, 16)
            sp.dma_start(bk[:, :], a["bk"]).then_inc(proj_loaded, 16)
            for n in range(1, NC):
                load_chunk(n)
            sp.dma_start(wv[:, :], a["wvT"]).then_inc(attn_consts_loaded, 16)
            sp.dma_start(bvr[0:1, :], a["bv"]).then_inc(attn_consts_loaded, 16)
            sp.dma_start(identb[:, :], a["ident_bf16"]).then_inc(attn_consts_loaded, 16)
            sp.dma_start(mask_qk[:, :], a["mask_qk"]).then_inc(attn_consts_loaded, 16)
            sp.dma_start(ident[:, :], a["ident"]).then_inc(attn_consts_loaded, 16)
            def load_rows(g):
                if g == GPB:
                    sp.wait_ge(parts_stored[1], 16 * NC)
                b, r = g // GPB, slice((g % GPB) * STRIP, (g % GPB + 1) * STRIP)
                s = g % NS
                for which, dst, reps in ((0, rows_q, None), (1, rows_k, 3)):
                    part = scr[which, b, :, r, :].rearrange("h (d j) t -> h d (j t)", d=D)
                    if reps is None:
                        spans = ((0, 24, part), (24, 16, part[0:2]), (40, 8, part[0]))
                    else:
                        spans = ((0, 24, part[0:1].to_broadcast([3, D, HG * T])),
                                 (24, 16, part[1:2].to_broadcast([2, D, HG * T])), (40, 8, part[2]))
                    for at, n, src in spans:
                        sp.dma_start(dst[at:at + n, s, :], src).then_inc(rows_loaded[s], 16)

            for n in range(2 * NC):
                q_or_k, n4 = n % 2, n // 2
                sp.wait_ge(parts_ready, n + 1)
                half_batch = slice((n4 % 2) * BANK, (n4 % 2 + 1) * BANK)
                sp.dma_start(scr[q_or_k, n4 // 2][:, :, half_batch].rearrange("h c t -> c h t"),
                             parts[:, n, :, :]).then_inc(parts_stored[n4 // 2], 16)
                if n == NC - 1:
                    sp.wait_ge(parts_stored[0], 16 * NC)
                    sp.wait_ge(slot0_cleared, 3)
                    load_rows(0)
            sp.wait_ge(slots_cleared, 3 * (NS - 1))
            for g in range(1, NS):
                load_rows(g)
            sp.dma_start(x[:, :, :], a["x"].rearrange("(n p) c -> p n c", p=P)).then_inc(tail_consts_loaded, 16)
            sp.dma_start(wo[:, :], a["woT"]).then_inc(tail_consts_loaded, 16)
            sp.dma_start(bob[:, :], a["bo"].to_broadcast([P, C])).then_inc(tail_consts_loaded, 16)
            sp.dma_start(gate_w[:, :], a["gateT"]).then_inc(tail_consts_loaded, 16)
            sp.dma_start(ebias[:, :], a["ebias"].to_broadcast([P, E])).then_inc(tail_consts_loaded, 16)

            def load_unit(u):
                if u >= 2:
                    sp.wait_ge(unit_split_steps, 2 * (u - 1))
                sp.dma_start(w_raw[:, u % 2, :], a["unitT"][:, u, :]).then_inc(unit_loaded[u % 2], 16)

            def store_max(g):
                s = g % NS
                sp.wait_ge(max_split, g + 1)
                for h in range(3):
                    sp.dma_start(rows_q[MROW + h:MROW + h + 1, s, :], mh[:, h, :]).then_inc(max_rows_loaded[s], 16)

            def store_output(n):
                sp.wait_ge(y_ready, QUAD * (n + 1))
                sp.dma_start(out[n * BANK:(n + 1) * BANK, :].rearrange("(t p) c -> p t c", p=P),
                             yy[:, n % 2, :, :]).then_inc(out_stored[n % 2], 16)

            u = 0
            for g in range(NG):
                store_max(g)
                if 1 <= g <= NG - NS:
                    sp.wait_ge(exp_scores, NE * g)
                    load_rows(g + NS - 1)
                for _ in range(3):
                    if u < NU:
                        load_unit(u)
                        u += 1

            sp.wait_ge(exp_scores, NE * (NG - 2))
            for n in range(NC):
                sp.wait_ge(comb_stored[n], 16)
                for u in range(NPAIR):
                    p, i = NPAIR * n + u, NU * n + 1 + u
                    if i in STORE_AT:
                        store_output(STORE_AT[i])
                    if p >= CB:
                        q = p - CB
                        sp.wait_ge(hidden_ready, q + q // NPAIR + 2)
                    for e in range(2):
                        sp.dma_start(comb_rows[e * I:(e + 1) * I, p % CB, :],
                                     a["weights"][2 * u + e:2 * u + e + 1, n * BANK:(n + 1) * BANK]
                                     .to_broadcast([I, BANK])).then_inc(comb_rows_loaded[p % CB], 16)
            store_output(NC - 2)
            store_output(NC - 1)
            for s in range(2):
                sp.wait_ge(out_stored[s], 16 * NC // 2)

        @block.gpsimd
        def _(pool):
            for s in range(1, NS):
                pool.memset(rows_q[0:MROW, s, :].bitcast(f32), 0.0).then_inc(slots_cleared, 1)
                pool.memset(rows_k[0:MROW, s, :].bitcast(f32), 0.0).then_inc(slots_cleared, 1)
                pool.wait_ge(slots_cleared, 3 * s - 1)
                pool.memset(rows_k[MROW:P, s, :].bitcast(f32), ONES).then_inc(slots_cleared, 1)
                pool.wait_ge(slots_cleared, 3 * s)
            pool.memset(half[:, :], -0.5).then_inc(consts_set, 1)
            pool.memset(Vg[:, :, :, :, :], 0.0).then_inc(consts_set, 1)
            pool.wait_ge(consts_set, 2)
            pool.memset(Vg[:, :, :, :, D:D + 1], 1.0).then_inc(consts_set, 1)
            pool.wait_ge(consts_set, 3)

            def values(g):
                pool.wait_ge(v_ready, 2 * (g // GPB + 1))
                if g >= 2:
                    pool.wait_ge(values_used, NV * (g - 1))
                c0 = (g % GPB) * STRIP
                src = V[:, (g // GPB) * KT:(g // GPB + 1) * KT, c0:c0 + STRIP]
                pool.tensor_copy(Vg[:, g % 2, :, :, 0:D],
                                 src.rearrange("p k (j d) -> p k j d", d=D)).then_inc(values_ready, 1)
                pool.wait_ge(values_ready, g + 1)

            def mask(g, kt):
                pool.wait_ge(exps_ready, NE * g + EXPS_UP_TO[kt])
                slot, c = PLACE[kt]
                v = probs[:, slot, :].rearrange("p (j t) -> p j t", j=HG)
                first_chunk = v[0:CHUNK, :, c + kt * P:c + (kt + 1) * P].rearrange("p j (c t) -> p j c t", c=2)
                second_chunk = v[CHUNK:P, :, c + kt * P + CHUNK:c + (kt + 1) * P]
                pool.affine_select(out=first_chunk, in_=first_chunk, compare_op=ALU.is_ge, fill=0.0, base=0,
                                   pattern=[[0, HG], [-2 * P, 2], [1, CHUNK]], channel_multiplier=-1).then_inc(squares_masked, 1)
                n = 2 * (KT * g + KT - 1 - kt)
                pool.wait_ge(squares_masked, n + 1)
                pool.affine_select(out=second_chunk, in_=second_chunk, compare_op=ALU.is_ge, fill=0.0, base=0,
                                   pattern=[[0, HG], [1, CHUNK]], channel_multiplier=-1).then_inc(squares_masked, 1)
                pool.wait_ge(squares_masked, n + 2)

            def split_unit(u):
                pool.wait_ge(unit_loaded[u % 2], 16 * (u // 2 + 1))
                pool.tensor_copy(w_hi[:, u, :], w_raw[:, u % 2, :]).then_inc(unit_split_steps, 1)
                pool.wait_ge(unit_split_steps, 2 * u + 1)
                pool.tensor_tensor(w_lo[:, u, :], w_raw[:, u % 2, :], w_hi[:, u, :],
                                   ALU.subtract).then_inc(unit_split_steps, 1)
                pool.wait_ge(unit_split_steps, 2 * u + 2)

            def root(n, at, k):
                pool.wait_ge(var_ready, n + 1)
                pool.tensor_tensor(rstd[:, at:at + k], ve[:, at:at + k], half[:, at:at + k],
                                   ALU.pow).then_inc(rstd_ready, 1)
                pool.wait_ge(rstd_ready, n + 1)

            values(0)
            pool.wait_ge(tail_consts_loaded, 16 * 5)
            pool.tensor_tensor(x[:, :, :], x[:, :, :], bob[:, :].unsqueeze(1).to_broadcast([P, NT, C]),
                               ALU.add).then_inc(x_biased, 1)
            pool.wait_ge(x_biased, 1)
            u = 0
            for g in range(NG):
                for kt in range(KT - 1, -1, -1):
                    mask(g, kt)
                    for q in range(2):
                        if KT * g + KT - kt == masks_before[q]:
                            root(q, q * QUAD, QUAD)
                    if kt == KT - 2 and g + 1 < NG:
                        values(g + 1)
                    if kt in (6, 5, 4) and u < NU:
                        split_unit(u)
                        u += 1

            def low_part(i):
                pool.wait_ge(hidden_high, i + 1)
                if i >= 2:
                    pool.wait_ge(down_done, i - 1)
                pool.tensor_tensor(hlo[:, i % 2, :], hh[:, i % 2, :], hhi[:, i % 2, :],
                                   ALU.subtract).then_inc(hidden_low, 1)

            for i in range(NC * NU):
                if i in ROOT_AT:
                    n, at_ = ROOT_AT[i]
                    root(n, at_, QUAD)
                low_part(i)
            root(*ROOT_AT[NC * NU], QUAD)

        @block.scalar
        def _(act):
            act.wait_ge(proj_loaded, 64)
            act.activation(bqs[:, :], bq[:, :], ACT.Copy, scale=scale[:, 0:1]).then_inc(bq_scaled, 1)
            act.wait_ge(bq_scaled, 1)
            for n in range(2 * NC):
                act.wait_ge(proj_done, n + 1)
                if n >= 2:
                    act.wait_ge(parts_ready, n - 1)
                how = dict(scale=scale[:, 0:1], bias=bqs[:, 0:1]) if n % 2 == 0 else dict(bias=bk[:, 0:1])
                act.activation(q32[:, n % 2, :], bank(n % 2), ACT.Identity, **how).then_inc(proj_copied, 1)
                act.activation(parts[:, n, 0, :], bank(n % 2), ACT.Identity, **how).then_inc(proj_copied, 1)

            for n in range(NC):
                act.wait_ge(v_projected, n + 1)
                act.copy(V[:, 4 * n:4 * n + 4, :], bank(2 + n).rearrange("p (t c) -> p t c", c=C)).then_inc(v_ready, 1)

            def exponentials(g, n):
                kt, j, per, stride = EXPU[n]
                cols = P * (kt + 1)
                act.wait_ge(exp_scores, NE * g + n + 1)
                pg, pk = PLACE_FROM[kt]
                if g + pg >= 0:
                    act.wait_ge(values_used, NV * (g + pg) + PIECES_UP_TO[pk])
                slot, c = PLACE[kt]
                src = ps[:, (n % 2) * 2 * BANK:(n % 2 + 1) * 2 * BANK]
                if per > 1:
                    src = src[:, 0:per * stride].rearrange("p (j n) -> p j n", j=per)[:, :, 0:cols]
                    dst = probs[:, slot, :].rearrange("p (j n) -> p j n", j=HG)[:, j:j + per, c:c + cols]
                else:
                    src = src[:, 0:cols]
                    dst = probs[:, slot, j * T + c:j * T + c + cols]
                act.activation(dst, src, ACT.Exp).then_inc(exps_ready, 1)

            def copy_output(g, h):
                act.wait_ge(values_used, NV * g + (UPPER_DONE if h else NV))
                act.copy(oT[:, g, h * BANK:(h + 1) * BANK], bank(4 + h)).then_inc(output_copied[h], 1)

            def tail_step(b, k):
                kind, q, _ = TAIL[k]
                n, (o, src) = 2 * b + q, tail_bank(b, k)
                if kind == "turn":
                    act.wait_ge(out_by_channel, n + 1)
                    act.copy(attT[:, :], src).then_inc(o, 1)
                elif kind == "x1T":
                    act.wait_ge(x1_by_channel, n + 1)
                    if n == 0:
                        act.wait_ge(values_ready, NG)
                    act.copy(x1hi[:, n * BANK:(n + 1) * BANK], src).then_inc(x1_high, 1)
                elif kind == "logit":
                    act.wait_ge(logits_ready, n + 1)
                    if n == 2:
                        act.wait_ge(comb_ready, 1)
                    first, second = ex[:, 0:QUAD * E], ex[:, QUAD * E:]
                    if q == 0:
                        act.copy(first, src[:, 0:QUAD * E]).then_inc(o, 1)
                    else:
                        act.activation(second, src[:, 0:QUAD * E], ACT.Exp, scale=-1.0).then_inc(o, 1)
                        k0 = TAIL.index(("logit", 0, 0))
                        act.wait_ge(tail_bank(b, k0)[0], tail_count(b, k0))
                        act.activation(first, first, ACT.Exp, scale=-1.0).then_inc(first_exps, 1)
                elif kind == "comb":
                    act.wait_ge(comb_by_expert, n + 1)
                    cols = slice(n * BANK, (n + 1) * BANK)
                    act.copy(combT[:, cols], src[0:E, :]).then_inc(o, 1)
                    act.wait_ge(o, tail_count(b, k))
                    act.dma_start(a["weights"][:, cols], combT[:, cols]).then_inc(comb_stored[n], 16)

            for kind, g, n in act_order:
                if kind == "x":
                    exponentials(g, n)
                elif kind == "c":
                    copy_output(g, n)
                else:
                    tail_step(g, n)

            def expert_sum(n):
                act.wait_ge(down_done, NU * (n + 1))
                if n >= 2:
                    act.wait_ge(sum_by_token, n - 1)
                act.copy(moT[:, n % 2, :], bank(ACC)).then_inc(sum_copied, 1)

            def high_part(i):
                act.wait_ge(hidden_ready, i + 1)
                if i >= 2:
                    act.wait_ge(down_done, i - 1)
                act.copy(hhi[:, i % 2, :], hh[:, i % 2, :]).then_inc(hidden_high, 1)

            for i in range(NC * NU + 1):
                if i >= NU and i % NU == 2:
                    expert_sum(i // NU - 1)
                if i - 1 in TAIL_AT:
                    tail_step(1, TAIL_AT[i - 1])
                if i < NC * NU:
                    act.wait_ge(gates_ready, i + 1)
                    if i >= 2:
                        wait_read(act, i - 2)
                    act.activation(sg[:, i % 2, :], bank(i % 2), ACT.Silu).then_inc(silu_ready, 1)
                if COMB + i < len(TAIL):
                    tail_step(0, COMB + i)
                if i >= 1:
                    high_part(i - 1)
            expert_sum(NC - 1)

        @block.vector
        def _(dve):
            dve.memset(ones[:, :], 1.0).then_inc(ones_set, 1)
            dve.memset(rows_q[0:MROW, 0, :].bitcast(f32), 0.0).then_inc(slot0_cleared, 1)
            dve.memset(rows_k[0:MROW, 0, :].bitcast(f32), 0.0).then_inc(slot0_cleared, 1)
            dve.memset(rows_k[MROW:P, 0, :].bitcast(f32), ONES).then_inc(slot0_cleared, 1)
            for n in range(2 * NC):
                s = n % 2
                dve.wait_ge(proj_copied, 2 * n + 2)
                dve.tensor_tensor(r32[:, s, :], q32[:, s, :], parts[:, n, 0, :], ALU.subtract).then_inc(split_steps, 1)
                dve.wait_ge(split_steps, 2 * n + 1)
                dve.tensor_copy(parts[:, n, 1, :], r32[:, s, :]).then_inc(split_steps, 1)
                dve.wait_ge(split_steps, 2 * n + 2)
                dve.tensor_tensor(parts[:, n, 2, :], r32[:, s, :], parts[:, n, 1, :],
                                  ALU.subtract).then_inc(parts_ready, 1)

            def maxima(g):
                for n, (cells, m, part) in enumerate(MAXU):
                    j, qt = cells[0][:2]
                    per = len(cells)
                    dve.wait_ge(max_scores, NM * g + n + 1)
                    src = bank(max_bank(g, n), per * m).rearrange("p (j m) -> p j m", j=per)
                    dve.tensor_reduce(mx[:, part, j:j + per, qt], src, AX.X, ALU.max).then_inc(max_read, 1)
                wide = KT - BANK // P
                dve.wait_ge(max_read, (NM - 1) * (g + 1))
                dve.tensor_tensor(mx[:, 0, :, 0:wide], mx[:, 0, :, 0:wide], mx[:, 1, :, 0:wide],
                                  ALU.max).then_inc(max_joined, 1)
                if g >= 1:
                    dve.wait_ge(max_rows_loaded[(g - 1) % NS], 48 * ((g - 1) // NS + 1))
                top = bank(TOP, P)[0:HG * KT, :]
                dve.wait_ge(max_scores, NM * (g + 1))
                dve.tensor_scalar(mh[:, 0, :], top, -1.0, None, ALU.mult).then_inc(max_split_steps, 1)
                dve.wait_ge(max_split_steps, 3 * g + 1)
                dve.scalar_tensor_tensor(mr[:, :], top, -1.0, mh[:, 0, :], ALU.mult,
                                         ALU.subtract).then_inc(max_split_steps, 1)
                dve.wait_ge(max_split_steps, 3 * g + 2)
                dve.tensor_copy(mh[:, 1, :], mr[:, :]).then_inc(max_split_steps, 1)
                dve.wait_ge(max_split_steps, 3 * g + 3)
                dve.tensor_tensor(mh[:, 2, :], mr[:, :], mh[:, 1, :], ALU.subtract).then_inc(max_split, 1)

            for g in range(NG):
                maxima(g)

            dve.wait_ge(tail_consts_loaded, 16 * 5)
            dve.tensor_copy(gate_hi[:, :], gate_w[:, :]).then_inc(gate_split, 1)
            dve.wait_ge(gate_split, 1)
            dve.tensor_tensor(gate_lo[:, :], gate_w[:, :], gate_hi[:, :], ALU.subtract).then_inc(gate_split, 1)
            dve.wait_ge(x_biased, 1)

            steps = [0]

            def steps_before(n):
                steps[0] += n
                return steps[0] - n

            def output(b, k):
                _, q, i = TAIL[k]
                t, (done, src) = KT * b + QUAD * q + i, tail_bank(b, k)
                o = src.rearrange("p (h e) -> p h e", e=STRIP)
                dve.wait_ge(out_by_token, t + 1)
                dve.reciprocal(rec[:, t % 2, :], o[:, :, D]).then_inc(sums_inverted, 1)
                dve.wait_ge(sums_inverted, t + 1)
                if i == 0 and t:
                    dve.wait_ge(out_by_channel, 2 * b + q)
                if t == 0:
                    dve.wait_ge(v_ready, NC)
                dve.tensor_tensor(att[:, i * C:(i + 1) * C].rearrange("p (h d) -> p h d", d=D), o[:, :, 0:D],
                                  rec[:, t % 2, :].unsqueeze(2).to_broadcast([P, HEADS, D]),
                                  ALU.mult).then_inc(done, 1)

            def residual(b, k):
                n, (done, src) = 2 * b + TAIL[k][1], tail_bank(b, k)
                dve.wait_ge(projected, n + 1)
                quad = x[:, QUAD * n:QUAD * (n + 1), :]
                dve.tensor_tensor(quad, src.rearrange("p (t c) -> p t c", c=C), quad, ALU.add).then_inc(done, 1)

            def statistics(b, k):
                n, (done, _) = 2 * b + TAIL[k][1], tail_bank(b, k)
                dve.wait_ge(done, tail_count(b, k))
                for t in range(QUAD * n, QUAD * (n + 1)):
                    dve.bn_stats(stats[:, t, :], x[:, t, :]).then_inc(stats_ready, 1)

            def aggregate(n, before):
                dve.wait_ge(stats_ready, before + QUAD)
                for t in range(QUAD * n, QUAD * (n + 1)):
                    dve.bn_aggr(mv[:, t, :], stats[:, t, :]).then_inc(moments_ready, 1)
                dve.wait_ge(moments_ready, before + QUAD)
                quad = slice(QUAD * n, QUAD * (n + 1))
                dve.tensor_scalar(ve[:, quad], mv[:, quad, 1], EPS, None, ALU.add).then_inc(var_ready, 1)

            def first_norm(n, before):
                dve.wait_ge(rstd_ready, before + 1)
                for t in range(QUAD * n, QUAD * (n + 1)):
                    dve.tensor_scalar(x[:, t, :], x[:, t, :], mv[:, t, 0:1], rstd[:, t:t + 1],
                                      ALU.subtract, ALU.mult).then_inc(x1_normed, 1)

            def x1_low(b, k):
                n, (done, src) = 2 * b + TAIL[k][1], tail_bank(b, k)
                dve.wait_ge(x1_high, n + 1)
                cols = slice(n * BANK, (n + 1) * BANK)
                dve.tensor_tensor(x1lo[:, cols], src, x1hi[:, cols], ALU.subtract).then_inc(done, 1)

            sc3, sfc3 = (v.rearrange("p (t e) -> p t e", e=E) for v in (sc, sfc))
            per = E // N_GROUP
            by_token = [P, KT, E]

            def router(b, n):
                if n == 0:
                    k = TAIL.index(("logit", 1, 0))
                    dve.wait_ge(tail_bank(b, k)[0], tail_count(b, k))
                    dve.wait_ge(first_exps, b + 1)
                    if b == 0:
                        dve.memset(gs[:, :, N_GROUP:], LAST).then_inc(router_steps, 1)
                        dve.memset(msk[:, :, E:], LAST).then_inc(router_steps, 1)
                        dve.wait_ge(router_steps, steps_before(2) + 2)
                    dve.tensor_scalar(ex, ex, 1.0, None, ALU.add).then_inc(router_steps, 1)
                    dve.wait_ge(router_steps, steps_before(1) + 1)
                    dve.reciprocal(sc, ex).then_inc(router_steps, 1)
                    steps_before(1)
                elif n == 1:
                    dve.wait_ge(router_steps, steps_before(1))
                    dve.tensor_tensor(sfc3, sc3, ebias[:, :].unsqueeze(1).to_broadcast(by_token),
                                      ALU.add).then_inc(router_steps, 1)
                    dve.wait_ge(router_steps, steps_before(1))
                    dve.tensor_reduce(gs[:, :, 0:N_GROUP], sfc.rearrange("p (t g e) -> p t g e", e=per, g=N_GROUP),
                                      AX.X, ALU.max).then_inc(router_steps, 1)
                elif n == 2:
                    dve.wait_ge(router_steps, steps_before(KT))
                    for t in range(KT):
                        dve.max(g8[:, t, :], gs[:, t, 0:N_GROUP]).then_inc(router_steps, 1)
                elif n == 3:
                    dve.wait_ge(router_steps, steps_before(1))
                    dve.memset(g8[:, :, TOPK_GROUP:], LAST).then_inc(router_steps, 1)
                    dve.wait_ge(router_steps, steps_before(KT))
                    for t in range(KT):
                        dve.match_replace(g_rest[:, t, :], g8[:, t, :], gs[:, t, :], LAST).then_inc(router_steps, 1)
                    dve.wait_ge(router_steps, steps_before(1))
                    dve.tensor_tensor(keep, gs[:, :, 0:N_GROUP], g_rest[:, :, 0:N_GROUP],
                                      ALU.not_equal).then_inc(router_steps, 1)
                    dve.wait_ge(router_steps, steps_before(1))
                    dve.tensor_tensor(msk[:, :, 0:E].rearrange("p t (g e) -> p t g e", e=per),
                                      sfc.rearrange("p (t g e) -> p t g e", e=per, g=N_GROUP),
                                      keep.unsqueeze(3).to_broadcast([P, KT, N_GROUP, per]),
                                      ALU.mult).then_inc(router_steps, 1)
                elif n == 4:
                    dve.wait_ge(router_steps, steps_before(KT))
                    for t in range(KT):
                        dve.max(m8[:, t, :], msk[:, t, 0:E]).then_inc(router_steps, 1)
                elif n == 5:
                    dve.wait_ge(router_steps, steps_before(1))
                    dve.memset(m8[:, :, TOP_K:], LAST).then_inc(router_steps, 1)
                    dve.wait_ge(router_steps, steps_before(KT))
                    for t in range(KT):
                        dve.match_replace(rest[:, t, :], m8[:, t, :], msk[:, t, :], LAST).then_inc(router_steps, 1)
                elif n == 6:
                    dve.wait_ge(router_steps, steps_before(1))
                    if b:
                        dve.wait_ge(comb_by_expert, 2)
                    dve.tensor_tensor(comb3, msk[:, :, 0:E], rest[:, :, 0:E], ALU.not_equal).then_inc(router_steps, 1)
                    dve.wait_ge(router_steps, steps_before(1))
                    dve.tensor_tensor(comb, comb, sc, ALU.mult).then_inc(router_steps, 1)
                elif n == 7:
                    dve.wait_ge(router_steps, steps_before(1))
                    dve.tensor_reduce(csum[:, :], comb3, AX.X, ALU.add).then_inc(router_steps, 1)
                    dve.wait_ge(router_steps, steps_before(1))
                    dve.tensor_scalar(csum[:, :], csum[:, :], 1e-20, None, ALU.add).then_inc(router_steps, 1)
                    dve.wait_ge(router_steps, steps_before(1))
                    dve.reciprocal(cs2[:, :], csum[:, :]).then_inc(router_steps, 1)
                    dve.wait_ge(router_steps, steps_before(0))
                    dve.scalar_tensor_tensor(comb3, comb3, ROUTE_SCALE,
                                             cs2[:, :].unsqueeze(2).to_broadcast(by_token),
                                             ALU.mult, ALU.mult).then_inc(comb_ready, 1)

            def tail(b, at):
                k = TAIL_AT.get(at - 1)
                if k is not None and TAIL[k][0] == "out":
                    output(b, k)
                elif k is not None and TAIL[k][0] == "proj":
                    residual(b, k)
                elif k is not None and TAIL[k][0] == "x1T":
                    x1_low(b, k)
                for q, first_at in enumerate(NORM_AT):
                    p = TAIL.index(("proj", q, 0))
                    n = 2 * b + q
                    if at == first_at:
                        statistics(b, p)
                    elif at == first_at + 1:
                        aggregate(n, QUAD * n)
                    elif at == first_at + 3:
                        first_norm(n, n)
                if ROUTER_AT <= at < ROUTER_AT + ROUTER_SLICES:
                    router(b, at - ROUTER_AT)

            for at_ in range(ROUTER_AT + ROUTER_SLICES):
                tail(0, at_)

            def second_sum(n):
                dve.wait_ge(sum_by_token, n + 1)
                if n >= 2:
                    dve.wait_ge(out_stored[n % 2], 16 * (n // 2))
                dve.tensor_tensor(yy[:, n % 2, :, :], bank(BACK).rearrange("p (t c) -> p t c", c=C),
                                  x[:, QUAD * n:QUAD * (n + 1), :], ALU.add).then_inc(y_summed, 1)

            def second_norm(n, step):
                if step == 0:
                    second_sum(n)
                elif step == 1:
                    dve.wait_ge(y_summed, n + 1)
                    for t in range(QUAD * n, QUAD * (n + 1)):
                        dve.bn_stats(stats[:, t, :], yy[:, n % 2, t % QUAD, :]).then_inc(stats_ready, 1)
                elif step == 2:
                    aggregate(n, QUAD * (4 + n))
                else:
                    dve.wait_ge(rstd_ready, (4 + n) + 1)
                    for t in range(QUAD * n, QUAD * (n + 1)):
                        y = yy[:, n % 2, t % QUAD, :]
                        dve.tensor_scalar(y, y, mv[:, t, 0:1], rstd[:, t:t + 1], ALU.subtract,
                                          ALU.mult).then_inc(y_ready, 1)

            for i in range(NC * NU):
                n, u = i // NU, i % NU
                if i < ROUTER_AT + ROUTER_SLICES:
                    tail(1, i)
                for first_at, m in SUM_AT.items():
                    if i - first_at in (0, 1, 2, 4):
                        second_norm(m, i - first_at)
                dve.wait_ge(silu_ready, i + 1)
                dve.wait_ge(ups_ready, i + 1)
                if i >= 2:
                    dve.wait_ge(hidden_low, i - 1)
                if u:
                    dve.tensor_tensor(au[:, i % 2, :], bank(2 + i % 2), sg[:, i % 2, :],
                                      ALU.mult).then_inc(gated_ready, 1)
                    dve.wait_ge(gated_ready, pairs(i + 1))
                    p = NPAIR * n + u - 1
                    dve.wait_ge(comb_rows_loaded[p % CB], 32 * (p // CB + 1))
                    dve.tensor_tensor(hh[:, i % 2, :], comb_rows[:, p % CB, :], au[:, i % 2, :],
                                      ALU.mult).then_inc(hidden_ready, 1)
                else:
                    dve.tensor_tensor(hh[:, i % 2, :], bank(2 + i % 2), sg[:, i % 2, :],
                                      ALU.mult).then_inc(hidden_ready, 1)
            for step in (0, 1, 2, 4):
                second_norm(NC - 1, step)

        @block.tensor
        def _(pe):
            pe.wait_ge(wq_loaded, 16)
            for n in range(2 * NC):
                if n == 1:
                    pe.wait_ge(proj_loaded, 64)
                if n % 2 == 0:
                    pe.wait_ge(xT_loaded[n // 2], 16)
                if n >= 2:
                    pe.wait_ge(proj_copied, 2 * (n - 1))
                n4 = n // 2
                pe.matmul(bank(n % 2), (wq, wk)[n % 2][:, :], xT[:, n4 * BANK:(n4 + 1) * BANK],
                          start=True, stop=True).then_inc(proj_done, 1)
            pe.wait_ge(attn_consts_loaded, 16 * 5)
            pe.wait_ge(ones_set, 1)
            for n in range(NC):
                for t in range(4):
                    tt = 4 * n + t
                    pe.matmul(bank(2 + n, P, t * P), xT[:, tt * P:(tt + 1) * P], wv[:, :],
                              start=True, stop=False)
                    mm = pe.matmul(bank(2 + n, P, t * P), ones[0:1, :], bvr[0:1, :], start=False, stop=True)
                mm.then_inc(v_projected, 1)

            def max_unit(g, n):
                s = g % NS
                if n == 0:
                    pe.wait_ge(rows_loaded[s], 96 * (g // NS + 1))
                if g == 0 and n == 2:
                    pe.wait_ge(proj_copied, 4 * NC)
                turn = len(FIRST_BANKS) if g == 0 else 2
                if n >= turn and n < NM - 1:
                    pe.wait_ge(max_read, (NM - 1) * g + n + 1 - turn)
                elif g >= 1 and n == 0:
                    pe.wait_ge(max_read, (NM - 1) * g)
                elif g >= 1:
                    pe.wait_ge(max_split_steps, 3 * g - 1)
                if n == NM - 1:
                    pe.wait_ge(max_joined, g + 1)
                    pe.transpose(bank(TOP, P)[0:HG * KT, :], mx[:, 0, :, :].rearrange("p j q -> p (j q)"),
                                 ident[:, :]).then_inc(max_scores, 1)
                    return
                cells, _, part = MAXU[n]
                for j, qt, k0, m, at in cells:
                    q = rows_q[0:K_MAX, s, j * T + qt * P:j * T + (qt + 1) * P]
                    mm = pe.matmul(bank(max_bank(g, n), m, at), q, rows_k[0:K_MAX, s, j * T + k0:j * T + k0 + m],
                                   start=True, stop=part == 1)
                    if part == 0:
                        mm = pe.matmul(bank(max_bank(g, n), P, at), identb[:, :], mask_qk[:, :], start=False,
                                       stop=True)
                mm.then_inc(max_scores, 1)

            def exp_unit(g, n):
                s = g % NS
                kt, j0, per, stride = EXPU[n]
                if n == 0:
                    pe.wait_ge(rows_loaded[s], 96 * (g // NS + 1))
                    pe.wait_ge(max_rows_loaded[s], 48 * (g // NS + 1))
                if g == 0 and n == 1:
                    pe.wait_ge(v_ready, NC)
                if NE * g + n >= 2:
                    pe.wait_ge(exps_ready, NE * g + n - 1)
                cols = P * (kt + 1)
                for a_ in range(per):
                    j = j0 + a_
                    base = (n % 2) * 2 * BANK + a_ * stride
                    k = rows_k[0:K_EXP, s, j * T + kt * P:j * T + (kt + 1) * P]
                    for c0 in range(0, cols, BANK):
                        m = min(BANK, cols - c0)
                        mm = pe.matmul(ps[:, base + c0:base + c0 + m], k,
                                       rows_q[0:K_EXP, s, j * T + c0:j * T + c0 + m],
                                       start=True, stop=True)
                mm.then_inc(exp_scores, 1)

            def values(g, n):
                kt, c0 = PIECES[n]
                if kt == KT - 1:
                    pe.wait_ge(values_ready, g + 1)
                    if g >= 1:
                        pe.wait_ge(output_copied[c0 // BANK], g)
                pe.wait_ge(exps_ready, NE * g + EXPS_UP_TO[kt])
                if n + 1 == PIECES_UP_TO[kt]:
                    pe.wait_ge(squares_masked, 2 * (KT * g + KT - kt))
                m = min(PIECE, P * (kt + 1) - c0)
                slot, c = PLACE[kt]
                for j in range(HG):
                    mm = pe.matmul(ps[STRIP * j:STRIP * (j + 1), 4 * BANK + c0:4 * BANK + c0 + m],
                                   Vg[:, g % 2, kt, j, :], probs[:, slot, j * T + c + c0:j * T + c + c0 + m],
                                   start=kt == KT - 1 and c0 % BANK == 0, stop=n + 1 in (UPPER_DONE, NV),
                                   tile_position=(0, STRIP * j), skip_group_check=True)
                mm.then_inc(values_used, 1)

            def tail_step(b, k):
                kind, q, i = TAIL[k]
                n, (done, dst) = 2 * b + q, tail_bank(b, k)
                if b == 0 and k < 2:
                    pe.wait_ge(*((max_read, (NM - 1) * NG) if k == 0 else (max_split_steps, 3 * NG - 1)))
                else:
                    pe.wait_ge(done, tail_count(b, k) - 1)
                if kind == "out":
                    if q == 0 and i == 0:
                        for h in range(2):
                            pe.wait_ge(output_copied[h], GPB * (b + 1))
                    t = QUAD * q + i
                    for g in range(GPB):
                        mm = pe.transpose(dst[:, g * P:(g + 1) * P], oT[:, b * GPB + g, t * P:(t + 1) * P],
                                          ident[:, :])
                    mm.then_inc(out_by_token, 1)
                elif kind == "turn":
                    last = TAIL.index(("out", q, QUAD - 1))
                    wait_step(pe, b, last)
                    wait_step(pe, b, last - 1)
                    for t in range(QUAD):
                        mm = pe.transpose(dst[:, t * P:(t + 1) * P], att[:, t * C:(t + 1) * C], ident[:, :])
                    mm.then_inc(out_by_channel, 1)
                elif kind == "proj":
                    wait_step(pe, b, TAIL.index(("turn", q, 0)))
                    for t in range(QUAD):
                        mm = pe.matmul(dst[:, t * P:(t + 1) * P], attT[:, t * P:(t + 1) * P], wo[:, :],
                                       start=True, stop=True)
                    mm.then_inc(projected, 1)
                elif kind == "x1T":
                    pe.wait_ge(x1_normed, QUAD * (n + 1))
                    for t in range(QUAD):
                        mm = pe.transpose(dst[:, t * P:(t + 1) * P], x[:, QUAD * n + t, :], ident[:, :])
                    mm.then_inc(x1_by_channel, 1)
                elif kind == "logit":
                    wait_step(pe, b, TAIL.index(("x1T", q, 0)))
                    pe.wait_ge(gate_split, 2)
                    for t in range(QUAD):
                        cols = slice((QUAD * n + t) * P, (QUAD * n + t + 1) * P)
                        o = dst[:, t * E:(t + 1) * E]
                        pe.matmul(o, x1hi[:, cols], gate_hi[:, :], start=True, stop=False)
                        pe.matmul(o, x1hi[:, cols], gate_lo[:, :], start=False, stop=False)
                        mm = pe.matmul(o, x1lo[:, cols], gate_hi[:, :], start=False, stop=True)
                    mm.then_inc(logits_ready, 1)
                else:
                    pe.wait_ge(comb_ready, b + 1)
                    for t in range(QUAD):
                        mm = pe.transpose(dst[0:E, t * P:(t + 1) * P], comb3[:, QUAD * q + t, :], ident[:, :])
                    mm.then_inc(comb_by_expert, 1)

            def up(i):
                n, u = i // NU, i % NU
                cols = slice(n * BANK, (n + 1) * BANK)
                for half_, dst, ready in ((0, bank(i % 2), gates_ready), (1, bank(2 + i % 2), ups_ready)):
                    if i >= 2 and half_ == 0:
                        pe.wait_ge(silu_ready, i - 1)
                    if i >= 2 and half_ == 1:
                        wait_read(pe, i - 2)
                    w = slice(half_ * P, (half_ + 1) * P)
                    pe.matmul(dst, w_hi[:, u, w], x1hi[:, cols], start=True, stop=False)
                    pe.matmul(dst, w_hi[:, u, w], x1lo[:, cols], start=False, stop=False)
                    pe.matmul(dst, w_lo[:, u, w], x1hi[:, cols], start=False, stop=True).then_inc(ready, 1)

            for kind, g, n in pe_order:
                if kind == "e":
                    exp_unit(g, n)
                elif kind == "m":
                    max_unit(g, n)
                elif kind == "v":
                    i = n - (NV - 3)
                    if g == NG - 1 and i in (0, 1):
                        if i == 0:
                            pe.wait_ge(unit_split_steps, 2 * NU)
                            pe.wait_ge(exps_ready, NE * NG)
                        up(i)
                    values(g, n)
                else:
                    tail_step(g, n)

            def down(i):
                n, u = i // NU, i % NU
                pe.wait_ge(hidden_low, i + 1)
                if u == 0 and n >= 1:
                    pe.wait_ge(sum_copied, n)
                w = slice(2 * P, 3 * P)
                pe.matmul(bank(ACC), w_hi[:, u, w], hhi[:, i % 2, :], start=u == 0, stop=False)
                pe.matmul(bank(ACC), w_lo[:, u, w], hhi[:, i % 2, :], start=False, stop=False)
                pe.matmul(bank(ACC), w_hi[:, u, w], hlo[:, i % 2, :], start=False,
                          stop=u == NU - 1).then_inc(down_done, 1)

            def back(n):
                pe.wait_ge(sum_copied, n + 1)
                if n == 0:
                    wait_step(pe, 1, TAIL.index(("comb", 1, 0)))
                else:
                    pe.wait_ge(y_summed, n)
                for t in range(QUAD):
                    mm = pe.transpose(bank(BACK, P, t * P), moT[:, n % 2, t * P:(t + 1) * P], ident[:, :])
                mm.then_inc(sum_by_token, 1)

            for k in range(COMB, len(TAIL)):
                tail_step(0, k)
            for h in range(2):
                pe.wait_ge(output_copied[h], NG)
            for i in range(NC * NU + 2):
                if 2 <= i < NC * NU:
                    up(i)
                if i in BACK_AT:
                    back(BACK_AT[i])
                if i >= 2:
                    down(i - 2)
                if i in TAIL_AT:
                    tail_step(1, TAIL_AT[i])
            back(NC - 1)


def kernel(**inputs):
    import numpy as np
    import ml_dtypes
    import concourse.bacc as bacc
    from concourse import mybir as mb
    from concourse.bass_utils import run_bass_kernel_spmd as run

    v = {k: np.asarray(a) for k, a in inputs.items()}

    def by_depth(w):
        return w.reshape(GPB, HG, D, -1).transpose(0, 2, 1, 3).reshape(C, -1)

    gate_up = v["L0_ffn_experts_gate_up"].reshape(NPAIR, 2, 2, I, C).transpose(4, 0, 2, 1, 3).reshape(C, NPAIR, 2 * P)
    shared = np.concatenate([v["L0_ffn_shared_gate_w"].T, v["L0_ffn_shared_up_w"].T], 1)[:, None, :]
    down = v["L0_ffn_experts_down"].reshape(NPAIR, 2, C, I).transpose(1, 3, 0, 2).reshape(P, NPAIR, C)
    tokens = v["L0_attn_x"].reshape(NTOK, C)
    at = np.arange(P)
    qb, kb = (at // CHUNK * CHUNK)[:, None], (at // CHUNK * CHUNK)[None, :]
    masked = (qb >= kb) & (at[None, :] - at[:, None] - 2 * (kb - qb) >= 1)
    mask = np.where(masked, np.float32(-3e38), np.float32(0)).astype(ml_dtypes.bfloat16)
    arrays = {
        "x": tokens, "xT": tokens.T,
        "wqT": by_depth(v["L0_attn_Wq"]).T, "wkT": by_depth(v["L0_attn_Wk"]).T,
        "wvT": v["L0_attn_Wv"].T, "woT": v["L0_attn_Wo"].T,
        "bq": by_depth(v["L0_attn_bq"]), "bk": by_depth(v["L0_attn_bk"]),
        "bv": v["L0_attn_bv"][None], "bo": v["L0_attn_bo"][None],
        "attn_scale": v["L0_attn_attn_scale"][None],
        "gateT": v["L0_ffn_gate_weight"].T, "ebias": v["L0_ffn_e_score_correction_bias"][None],
        "unitT": np.concatenate([np.concatenate([shared, gate_up], 1),
                                 np.concatenate([v["L0_ffn_shared_down_w"].T[:, None, :], down], 1)], 2),
        "ident": np.eye(P, dtype=np.float32), "ident_bf16": np.eye(P, dtype=ml_dtypes.bfloat16),
        "mask_qk": mask,
    }
    nc = bacc.Bacc("TRN2", target_bir_lowering=False, num_devices=1)
    feeds, a = {}, {}
    for name, array in arrays.items():
        array = np.ascontiguousarray(array)
        feeds[f"in_{name}"] = array
        a[name] = nc.dram_tensor(f"in_{name}", array.shape, mb.dt.from_np(array.dtype), kind="ExternalInput").ap()
    a["scratch"] = nc.dram_tensor("scratch", (2, B, 3, C, T), mb.dt.bfloat16).ap()
    a["weights"] = nc.dram_tensor("weights", (E, NTOK), mb.dt.float32).ap()
    out = nc.dram_tensor("out", (NTOK, C), mb.dt.float32, kind="ExternalOutput").ap()
    build(nc, a, out)
    r = run(nc, [feeds], core_ids=[0])
    return r.results[0]["out"].reshape(B, T, C)
```
